# Optimizing a Trainium2 kernel written in Bass

```python
import numpy as np
import jax
import jax.numpy as jnp

def _softmax(x, axis=-1):
    return jax.nn.softmax(x, axis=axis)

def _gelu(x):
    return jax.nn.gelu(x, approximate=True)

def _silu(x):
    return jax.nn.silu(x)

def _sigmoid(x):
    return jax.nn.sigmoid(x)

def _layernorm(x, axis=-1, eps=1e-05):
    m = jnp.mean(x, axis=axis, keepdims=True)
    v = jnp.var(x, axis=axis, keepdims=True)
    return (x - m) / jnp.sqrt(v + eps)

def _scatter_add(tgt, idx, src, axis=0):
    return tgt.at[idx].add(src)

def _segment_sum(src, seg, n):
    return jax.ops.segment_sum(src, seg, n)
kernel_name = 'mk_gnn_resnorm_d1_gnn_r8_e929a3'

def setup_inputs(seed: int=0):
    np.random.seed(seed)
    _w = jnp.asarray

    def _rec_inputs():
        import jax
        import jax.numpy as jnp
        _gk = jax.random.key(seed)
        x = -0.000202 + 1 * jax.random.normal(jax.random.fold_in(_gk, 1), (12500, 64), jnp.float32)
        _s = jax.random.randint(jax.random.fold_in(_gk, 2), (200000,), 0, 12500, jnp.int32)
        _d = jax.random.randint(jax.random.fold_in(_gk, 3), (200000,), 0, 12500, jnp.int32)
        _loop = jnp.arange(12500, dtype=jnp.int32)
        src = jnp.concatenate([_s, _d, _loop])
        dst = jnp.concatenate([_d, _s, _loop])
        _o = jnp.argsort(dst, stable=True)
        src = src[_o]
        dst = dst[_o]
        edge_attr_18 = 0.000175535 + 1.00015 * jax.random.normal(jax.random.fold_in(_gk, 11), (412500, 18), jnp.float32)
        return (x, src, dst, edge_attr_18)
    x, src, dst, edge_attr_18 = _rec_inputs()

    def _L0_gnn_setup():
        import jax, jax.numpy as jnp
        import numpy as np
        N = 12500
        E = 200000
        DIM = 64
        H = 4
        D = 8
        DH = D * H
        VD = DIM // H
        RPE_IN = 18
        key = jax.random.key(seed)
        ks = jax.random.split(key, 12)
        x = jax.random.normal(ks[0], (N, DIM), dtype=jnp.float32)
        edge_index = jax.random.randint(ks[1], (2, E), 0, N, dtype=jnp.int64)
        edge_attr = jax.random.normal(ks[2], (E, RPE_IN), dtype=jnp.float32)
        sc = lambda fan_in: 1.0 / np.sqrt(fan_in)
        qkv_w = jax.random.uniform(ks[3], (DIM, 2 * DH + DIM), jnp.float32, -sc(DIM), sc(DIM))
        qkv_b = jax.random.uniform(ks[4], (2 * DH + DIM,), jnp.float32, -sc(DIM), sc(DIM))
        k_rpe_w = jax.random.uniform(ks[5], (RPE_IN, DH), jnp.float32, -sc(RPE_IN), sc(RPE_IN))
        k_rpe_b = jax.random.uniform(ks[6], (DH,), jnp.float32, -sc(RPE_IN), sc(RPE_IN))
        q_rpe_w = jax.random.uniform(ks[7], (RPE_IN, DH), jnp.float32, -sc(RPE_IN), sc(RPE_IN))
        q_rpe_b = jax.random.uniform(ks[8], (DH,), jnp.float32, -sc(RPE_IN), sc(RPE_IN))
        v_rpe_w = jax.random.uniform(ks[9], (RPE_IN, DIM), jnp.float32, -sc(RPE_IN), sc(RPE_IN))
        v_rpe_b = jax.random.uniform(ks[10], (DIM,), jnp.float32, -sc(RPE_IN), sc(RPE_IN))
        return {'x': x, 'edge_index': edge_index, 'edge_attr': edge_attr, 'qkv_w': qkv_w, 'qkv_b': qkv_b, 'k_rpe_w': k_rpe_w, 'k_rpe_b': k_rpe_b, 'q_rpe_w': q_rpe_w, 'q_rpe_b': q_rpe_b, 'v_rpe_w': v_rpe_w, 'v_rpe_b': v_rpe_b}
    _L0_gnn_all = _L0_gnn_setup()
    _L0_gnn_in = {k: v for k, v in _L0_gnn_all.items() if k in ('qkv_w', 'qkv_b', 'k_rpe_w', 'k_rpe_b', 'q_rpe_w', 'q_rpe_b', 'v_rpe_w', 'v_rpe_b')}
    del _L0_gnn_all
    return {'x': x, 'src': src, 'dst': dst, 'edge_attr_18': edge_attr_18, 'L0_gnn_qkv_w': _L0_gnn_in['qkv_w'], 'L0_gnn_qkv_b': _L0_gnn_in['qkv_b'], 'L0_gnn_k_rpe_w': _L0_gnn_in['k_rpe_w'], 'L0_gnn_k_rpe_b': _L0_gnn_in['k_rpe_b'], 'L0_gnn_q_rpe_w': _L0_gnn_in['q_rpe_w'], 'L0_gnn_q_rpe_b': _L0_gnn_in['q_rpe_b'], 'L0_gnn_v_rpe_w': _L0_gnn_in['v_rpe_w'], 'L0_gnn_v_rpe_b': _L0_gnn_in['v_rpe_b']}

def reference(x, src, dst, edge_attr_18, L0_gnn_qkv_w, L0_gnn_qkv_b, L0_gnn_k_rpe_w, L0_gnn_k_rpe_b, L0_gnn_q_rpe_w, L0_gnn_q_rpe_b, L0_gnn_v_rpe_w, L0_gnn_v_rpe_b):
    import jax
    import jax.numpy as jnp

    def _L0_gnn_ref(x, edge_index, edge_attr, qkv_w, qkv_b, k_rpe_w, k_rpe_b, q_rpe_w, q_rpe_b, v_rpe_w, v_rpe_b):
        import jax, jax.numpy as jnp
        import numpy as np
        N = 12500
        E = 200000
        DIM = 64
        H = 4
        D = 8
        DH = D * H
        VD = DIM // H
        RPE_IN = 18
        n = x.shape[0]
        e = edge_index.shape[1]
        qkv = x @ qkv_w + qkv_b
        q = qkv[:, :DH].reshape(n, H, D)
        k = qkv[:, DH:2 * DH].reshape(n, H, D)
        v = qkv[:, 2 * DH:].reshape(n, H, VD)
        s = edge_index[0]
        t = edge_index[1]
        scale = jnp.float32(D) ** (-0.5)
        qe = q[s] * scale
        qe = qe + (edge_attr @ q_rpe_w + q_rpe_b).reshape(e, H, D)
        ke = k[t] + (edge_attr @ k_rpe_w + k_rpe_b).reshape(e, H, D)
        ve = v[t] + (edge_attr @ v_rpe_w + v_rpe_b).reshape(e, H, VD)
        compat = jnp.einsum('ehd,ehd->eh', qe, ke)
        m = jax.ops.segment_max(compat, s, num_segments=n)
        ex = jnp.exp(compat - m[s])
        den = jax.ops.segment_sum(ex, s, num_segments=n)
        attn = ex / (den[s] + 1e-16)
        msg = (ve * attn[..., None]).reshape(e, DIM)
        out = jax.ops.segment_sum(msg, s, num_segments=n)
        return out
    edge_index = jnp.stack([src, dst])
    x = _layernorm(x + _L0_gnn_ref(x, edge_index, edge_attr_18, L0_gnn_qkv_w, L0_gnn_qkv_b, L0_gnn_k_rpe_w, L0_gnn_k_rpe_b, L0_gnn_q_rpe_w, L0_gnn_q_rpe_b, L0_gnn_v_rpe_w, L0_gnn_v_rpe_b), axis=-1)
    return x

_drawn_inputs = setup_inputs


def setup_inputs(seed=0):
    import zlib

    import numpy as np

    out = dict(_drawn_inputs(seed))
    spreads = {}
    factors = {}
    for name, (base, spread) in spreads.items():
        noise = np.random.default_rng([zlib.crc32(name.encode()), seed]).standard_normal(out[name].shape)
        drawn = base * np.exp(spread * noise) if base else spread * noise
        out[name] = jnp.asarray(drawn.astype(out[name].dtype))
    for name, factor in factors.items():
        out[name] = (out[name] * factor).astype(out[name].dtype)
    return out
```

```python
import math
from contextlib import ExitStack

import numpy as np
import concourse.bass as bass
from concourse import mybir

F32 = mybir.dt.float32
BF16 = mybir.dt.bfloat16
I32 = mybir.dt.int32
ALU = mybir.AluOpType
ACT = mybir.ActivationFunctionType
AX = mybir.AxisListType

P = 128
N, E = 12500, 412500
DIM, H, D = 64, 4, 8
DH, VD = H * D, DIM // H
ATTR = 18
NB = math.ceil(N / P)
NN = NB * P
CT = 4
CE = CT * P
NS = 2
HALF = 2
NCH = math.ceil(E / (CE * NS * HALF)) * NS * HALF
EP = NCH * CE
NT = NCH * CT
SC = NCH // NS
TURNS = SC // HALF
TT = NS * HALF * CT
KV = DH + DIM
REC = KV + H
WP = 101
WG = NCH // WP
K_ROWS = CT * ATTR + 1
BIG = 1.0e30
S0 = 56
SX = 16
RROWS = EP + S0 + SX
XG = 7
R_EQ = 4
assert WP * WG == NCH and NCH % (NS * HALF) == 0 and NB % (2 * XG) == 0 and TT % R_EQ == 0


def row_of(v):
    return v.rearrange("(a n) -> a n", a=1)


def gnn_kernel(nc, x, xT, src_lin, src_tiles, dst_lin, dst_tiles, attr, qkv_w, qkv_b, k_rpe_w, k_rpe_b,
               q_rpe_w, q_rpe_b, v_rpe_w, v_rpe_b, out):
    lo_dram = nc.dram_tensor("lo_dram", (NCH, CE), BF16, kind="Internal").ap()
    dl_dram = nc.dram_tensor("dl_dram", (NCH, CE), BF16, kind="Internal").ap()
    win_dram = nc.dram_tensor("win_dram", (NCH,), I32, kind="Internal").ap()
    over_dram = nc.dram_tensor("over_dram", (NCH,), F32, kind="Internal").ap()
    kv_dram = nc.dram_tensor("kv_dram", (NN, KV), F32, kind="Internal").ap()
    rec_dram = nc.dram_tensor("rec_dram", (RROWS, REC), F32, kind="Internal").ap()

    with ExitStack() as keep:
        def kept(name, shape, dt=F32):
            return keep.enter_context(nc.sbuf_tensor(name, shape, dt))

        T = dict(
            iota_row=kept("iota_row", [P, P], BF16),
            iota_f=kept("iota_f", [P, P]),
            iota_p=kept("iota_p", [P, 1]),
            ident=kept("ident", [P, P]),
            later=kept("later", [P, P]),
            lo_f=kept("lo_f", [P, NT]),
            hi_f=kept("hi_f", [P, NT]),
            q_tab=kept("q_tab", [P, NB, DH]),
            base=kept("base", [P, NS, NB]),
            deg=kept("deg", [P, NB]),
            w_attr=kept("w_attr", [P, CT, KV + DH]),
            win_row=kept("win_row", [1, NCH], I32),
            flag=kept("flag", [1, 1], I32),
        )
        tables_stage(nc, T, xT, src_lin, src_tiles, dst_lin, qkv_w, qkv_b, k_rpe_w, k_rpe_b,
                     q_rpe_w, q_rpe_b, v_rpe_w, v_rpe_b, lo_dram, dl_dram, win_dram, over_dram, kv_dram,
                     rec_dram)
        sort_stage(nc, T, attr, dst_tiles, lo_dram, dl_dram, kv_dram, rec_dram)
        attend_stage(nc, T, x, rec_dram, out)


def tables_stage(nc, T, xT, src_lin, src_tiles, dst_lin, qkv_w, qkv_b, k_rpe_w, k_rpe_b,
                 q_rpe_w, q_rpe_b, v_rpe_w, v_rpe_b, lo_dram, dl_dram, win_dram, over_dram, kv_dram,
                 rec_dram):
    iota_row, iota_f, iota_p, ident, later = (T[k] for k in ("iota_row", "iota_f", "iota_p", "ident", "later"))
    lo_f, hi_f, q_tab, base, deg, w_attr = (T[k] for k in ("lo_f", "hi_f", "q_tab", "base", "deg", "w_attr"))
    win_row, flag = T["win_row"], T["flag"]
    RING = 8
    with ExitStack() as ctx:
        def sb(name, shape, dt=F32):
            return ctx.enter_context(nc.sbuf_tensor(name, shape, dt))

        def sem(name):
            return ctx.enter_context(nc.semaphore(name))

        iota_i = sb("iota_i", [P, P], I32)
        iota_pi = sb("iota_pi", [P, 1], I32)
        src_i = sb("src_i", [P, NT], I32)
        dig_i = sb("dig_i", [P, NT], I32)
        srcl_i = sb("srcl_i", [P, NT], I32)
        lo_lin = sb("lo_lin", [P, NT], BF16)
        dst_l = sb("dst_l", [WP, WG, CE], I32)
        dst_loc = sb("dst_loc", [WP, WG, CE], BF16)
        win_f = sb("win_f", [WP, WG])
        win_i = sb("win_i", [WP, WG], I32)
        over = sb("over", [WP, WG])
        over_row = sb("over_row", [1, NCH])
        flag_f = sb("flag_f", [1, 1])
        ones = sb("ones", [P, NB])
        incl = sb("incl", [P, NB])
        row_base = sb("row_base", [P, 1])
        h_lo = sb("h_lo", [P, RING, P], BF16)
        h_hi = sb("h_hi", [P, RING, NB], BF16)
        w_qkv = sb("w_qkv", [DIM + 1, 2 * DH + DIM])
        xt = [sb(f"xt{i}", [DIM + 1, XG * P]) for i in range(2)]
        kvt = sb("kvt", [P, NB, KV])
        tail = sb("tail", [S0 + SX, REC])
        ps_hist = ctx.enter_context(nc.psum_tensor("ps_hist", [P, NS, 256], F32))
        ps_row = ctx.enter_context(nc.psum_tensor("ps_row", [P, 512], F32))
        ps_x = [ctx.enter_context(nc.psum_tensor(f"ps_x{i}", [P, 8, P], F32)) for i in range(2)]

        src_in, srcl_in, dst_in = sem("src_in"), sem("srcl_in"), sem("dst_in")
        w_zero, w_in, x_ones = sem("w_zero"), sem("w_in"), sem("x_ones")
        iotas, consts, diag = sem("iotas"), sem("consts"), sem("diag")
        steps = sem("steps")
        lo_made, lo_out = sem("lo_made"), sem("lo_out")
        loc_made, loc_out = sem("loc_made"), sem("loc_out")
        win_made, win_out, win_in, flag_made = sem("win_made"), sem("win_out"), sem("win_in"), sem("flag_made")
        hot, tally_slots = sem("hot"), sem("tally_slots")
        sums_made, rows_summed = sem("sums_made"), sem("rows_summed")
        tail_zero, tail_out = sem("tail_zero"), sem("tail_out")
        x_in = [sem(f"x_in{i}") for i in range(2)]
        x_done, q_read = sem("x_done"), sem("q_read")
        kv_read = sem("kv_read")
        kv_out = sem("kv_out")
        n_w = 2 + 6 * CT

        block = ctx.enter_context(nc.Block())

        @block.sync
        def _(sp):
            sp.dma_start(src_i[:, :], src_tiles).then_inc(src_in, 16)
            sp.dma_start(srcl_i[:, :], src_lin.rearrange("(p t) -> p t", p=P)).then_inc(srcl_in, 16)
            sp.dma_start(dst_l[:, :, :], dst_lin.rearrange("(p g e) -> p g e", p=WP, g=WG)).then_inc(dst_in, 16)
            sp.dma_start(w_qkv[0:DIM, :], qkv_w).then_inc(w_in, 16)
            sp.dma_start(w_qkv[DIM:DIM + 1, :], row_of(qkv_b)).then_inc(w_in, 16)
            sp.wait_ge(w_zero, 1)
            for j in range(CT):
                for c, w, b in ((0, k_rpe_w, k_rpe_b), (DH, v_rpe_w, v_rpe_b), (KV, q_rpe_w, q_rpe_b)):
                    n = w.shape[1]
                    sp.dma_start(w_attr[ATTR * j:ATTR * (j + 1), j, c:c + n], w).then_inc(w_in, 16)
                    sp.dma_start(w_attr[K_ROWS - 1:K_ROWS, j, c:c + n], row_of(b)).then_inc(w_in, 16)
            sp.wait_ge(x_ones, 2)
            with sp.Fori(0, NB // (2 * XG)) as it:
                for i in range(2):
                    sp.wait_ge(x_done, 2 * it + i + 1)
                    sp.dma_start(xt[i][0:DIM, :], xT[:, bass.ds((2 * it + i) * XG * P, XG * P)]).then_inc(x_in[i], 16)
            sp.wait_ge(lo_made, 1)
            sp.dma_start(lo_dram.rearrange("c e -> (c e)").rearrange("(p t) -> p t", p=P), lo_lin[:, :]).then_inc(lo_out, 16)
            sp.wait_ge(loc_made, WG)
            sp.dma_start(dl_dram.rearrange("(p g) e -> p g e", p=WP), dst_loc[:, :, :]).then_inc(loc_out, 16)
            sp.wait_ge(win_made, 2)
            sp.dma_start(win_dram.rearrange("(p g) -> p g", p=WP), win_i[:, :]).then_inc(win_out, 16)
            sp.dma_start(over_dram.rearrange("(p g) -> p g", p=WP), over[:, :]).then_inc(win_out, 16)
            sp.wait_ge(win_out, 32)
            sp.dma_start(win_row[:, :], row_of(win_dram)).then_inc(win_in, 16)
            sp.dma_start(over_row[:, :], row_of(over_dram)).then_inc(win_in, 16)
            sp.wait_ge(kv_read, NB // XG)
            sp.dma_start(kv_dram.rearrange("(b p) f -> p b f", p=P), kvt[:, :, :]).then_inc(kv_out, 16)
            sp.wait_ge(kv_out, 16)
            sp.wait_ge(tail_zero, 1)
            sp.dma_start(rec_dram[EP:RROWS, :], tail[:, :]).then_inc(tail_out, 16)
            sp.wait_ge(tail_out, 16)
            sp.wait_ge(lo_out, 16)
            sp.wait_ge(loc_out, 16)
            sp.wait_ge(win_in, 32)
            sp.wait_ge(w_in, 16 * n_w)

        @block.gpsimd
        def _(pool):
            pool.iota(iota_i[:, :], pattern=[[1, P]], base=0, channel_multiplier=0).then_inc(iotas, 1)
            pool.iota(iota_pi[:, :], pattern=[[0, 1]], base=0, channel_multiplier=1).then_inc(iotas, 1)
            pool.memset(ident[:, :], 0.0).then_inc(diag, 1)
            pool.memset(later[:, :], 1.0).then_inc(diag, 1)
            pool.wait_ge(diag, 2)
            pool.affine_select(out=ident[:, :], in_=ident[:, :], compare_op=ALU.not_equal, fill=1.0,
                               base=0, pattern=[[-1, P]], channel_multiplier=1).then_inc(diag, 1)
            pool.affine_select(out=later[:, :], in_=later[:, :], compare_op=ALU.is_gt, fill=0.0,
                               base=0, pattern=[[1, P]], channel_multiplier=-1).then_inc(diag, 1)
            pool.wait_ge(diag, 4)

        @block.vector
        def _(dve):
            dve.memset(w_attr[:, :, :], 0.0).then_inc(w_zero, 1)
            dve.memset(xt[0][DIM:DIM + 1, :], 1.0).then_inc(x_ones, 1)
            dve.memset(xt[1][DIM:DIM + 1, :], 1.0).then_inc(x_ones, 1)
            dve.memset(tail[:, :], 0.0).then_inc(tail_zero, 1)
            dve.memset(ones[:, :], 1.0).then_inc(consts, 1)
            dve.wait_ge(iotas, 2)
            dve.tensor_copy(iota_row[:, :], iota_i[:, :]).then_inc(consts, 1)
            dve.tensor_copy(iota_f[:, :], iota_i[:, :]).then_inc(consts, 1)
            dve.tensor_copy(iota_p[:, :], iota_pi[:, :]).then_inc(consts, 1)
            n = 0

            def step(ins):
                nonlocal n
                n += 1
                ins.then_inc(steps, 1)
                dve.wait_ge(steps, n)

            dve.wait_ge(src_in, 16)
            step(dve.tensor_single_scalar(dig_i[:, :], src_i[:, :], P - 1, ALU.bitwise_and))
            step(dve.tensor_copy(lo_f[:, :], dig_i[:, :]))
            step(dve.tensor_single_scalar(dig_i[:, :], src_i[:, :], 7, ALU.arith_shift_right))
            step(dve.tensor_copy(hi_f[:, :], dig_i[:, :]))
            dve.wait_ge(consts, 4)
            with dve.Fori(0, NT // RING) as it:
                for k in range(RING):
                    dve.wait_ge(tally_slots, RING * it + k + 1)
                    t = RING * it + k
                    dve.tensor_scalar(h_lo[:, k, :], iota_row[:, :], lo_f[:, bass.ds(t, 1)], None, ALU.is_equal)
                    dve.tensor_scalar(h_hi[:, k, :], iota_row[:, 0:NB], hi_f[:, bass.ds(t, 1)], None,
                                      ALU.is_equal).then_inc(hot, 1)
            dve.wait_ge(srcl_in, 16)
            step(dve.tensor_single_scalar(dig_i[:, :], srcl_i[:, :], P - 1, ALU.bitwise_and))
            dve.tensor_copy(lo_lin[:, :], dig_i[:, :]).then_inc(lo_made, 1)
            dve.wait_ge(dst_in, 16)
            step(dve.tensor_reduce(win_f[:, :], dst_l[:, :, :], AX.X, ALU.min))
            step(dve.tensor_single_scalar(win_f[:, :], win_f[:, :], float(NN - P), ALU.min))
            step(dve.tensor_reduce(over[:, :], dst_l[:, :, :], AX.X, ALU.max))
            dve.tensor_copy(win_i[:, :], win_f[:, :]).then_inc(win_made, 1)
            dve.tensor_sub(over[:, :], over[:, :], win_f[:, :]).then_inc(win_made, 1)
            for g in range(WG):
                dve.tensor_scalar(dst_loc[:, g, :], dst_l[:, g, :], win_f[:, g:g + 1], None,
                                  ALU.subtract).then_inc(loc_made, 1)
            dve.wait_ge(win_in, 32)
            step(dve.reduce_max(flag_f[:, :], over_row[:, :], AX.X))
            step(dve.tensor_single_scalar(flag_f[:, :], flag_f[:, :], float(P), ALU.is_ge))
            dve.tensor_copy(flag[:, :], flag_f[:, :]).then_inc(flag_made, 1)
            dve.wait_ge(tally_slots, RING + NT)
            step(dve.tensor_copy(base[:, :, :], ps_hist[:, :, 0:NB]))
            step(dve.tensor_add(deg[:, :], base[:, 0, :], base[:, 1, :]))
            step(dve.tensor_tensor_scan(incl[:, :], ones[:, :], deg[:, :], 0.0, ALU.mult, ALU.add))
            sums = dve.tensor_sub(incl[:, 0:NB - 1], incl[:, 0:NB - 1], deg[:, 0:NB - 1])
            sums.then_inc(sums_made, 1)
            dve.wait_ge(sums_made, 1)
            dve.wait_ge(rows_summed, 1)
            step(dve.tensor_copy(row_base[:, :], ps_row[:, 0:1]))
            step(dve.tensor_sub(incl[:, NB - 1:NB], incl[:, NB - 1:NB], deg[:, NB - 1:NB]))
            step(dve.tensor_scalar(incl[:, :], incl[:, :], row_base[:, 0:1], None, ALU.add))
            step(dve.tensor_add(base[:, 1, :], base[:, 0, :], incl[:, :]))
            step(dve.tensor_copy(base[:, 0, :], incl[:, :]))
            dve.wait_ge(loc_made, WG)
            dve.wait_ge(flag_made, 1)
            dve.wait_ge(lo_made, 1)

        @block.tensor
        def _(pe):
            pe.sem_inc(tally_slots, RING)
            pe.sem_inc(x_done, 2)
            for s in range(NS):
                for k in range(RING):
                    pe.wait_ge(hot, NT // NS * s + k + 1)
                    nc.tensor.matmul(ps_hist[:, s, 0:NB], h_lo[:, k, :], h_hi[:, k, :], start=(s == 0 and k == 0),
                                     stop=False, skip_group_check=True).then_inc(tally_slots, 1)
                with pe.Fori(1, NT // NS // RING) as it:
                    for k in range(RING):
                        pe.wait_ge(hot, NT // NS * s + RING * it + k + 1)
                        nc.tensor.matmul(ps_hist[:, s, 0:NB], h_lo[:, k, :], h_hi[:, k, :], start=False,
                                         stop=False, skip_group_check=True).then_inc(tally_slots, 1)
            pe.wait_ge(w_in, 16 * n_w)
            with pe.Fori(0, NB // (2 * XG)) as it:
                for i in range(2):
                    pe.wait_ge(x_in[i], 16 * it + 16)
                    pe.wait_ge(q_read, 2 * it + i + 1)
                    for b in range(XG):
                        last = nc.tensor.matmul(ps_x[i][:, b, :], xt[i][:, b * P:(b + 1) * P], w_qkv[:, :],
                                                start=True, stop=True)
                    last.then_inc(x_done, 1)
            pe.wait_ge(sums_made, 1)
            pe.wait_ge(diag, 4)
            nc.tensor.matmul(ps_row[:, 0:1], later[:, :], incl[:, NB - 1:NB], start=True,
                             stop=True).then_inc(rows_summed, 1)

        @block.scalar
        def _(act):
            act.sem_inc(q_read, 2)
            with act.Fori(0, NB // (2 * XG)) as it:
                for i in range(2):
                    act.wait_ge(x_done, 2 + 2 * it + i + 1)
                    act.activation(kvt[:, bass.ds((2 * it + i) * XG, XG), :], ps_x[i][:, 0:XG, DH:DH + KV], ACT.Copy).then_inc(kv_read, 1)
                    act.activation(q_tab[:, bass.ds((2 * it + i) * XG, XG), :], ps_x[i][:, 0:XG, 0:DH], ACT.Copy,
                                   scale=float(D) ** -0.5).then_inc(q_read, 1)


def sort_stage(nc, T, attr, dst_tiles, lo_dram, dl_dram, kv_dram, rec_dram):
    iota_row, iota_f, iota_p, ident, later = (T[k] for k in ("iota_row", "iota_f", "iota_p", "ident", "later"))
    lo_f, hi_f, base, w_attr, win_row, flag = (T[k] for k in ("lo_f", "hi_f", "base", "w_attr", "win_row", "flag"))
    UNITS = [(u, s) for u in range(HALF) for s in range(NS)]
    with ExitStack() as ctx:
        def sb(name, shape, dt=F32):
            return ctx.enter_context(nc.sbuf_tensor(name, shape, dt))

        def sem(name):
            return ctx.enter_context(nc.semaphore(name))

        NU = len(UNITS)
        dst_i = sb("dst_i", [P, NT], I32)
        lo_b = [sb(f"lo_b{c}", [P, CE], BF16) for c in range(NU)]
        dst_b = [sb(f"dst_b{c}", [P, CE], BF16) for c in range(NU)]
        at = [sb(f"at{c}", [P, P]) for c in range(NU)]
        kvw = [sb(f"kvw{c}", [P, KV]) for c in range(NU)]
        kvg = [sb(f"kvg{c}", [P, CT, KV]) for c in range(NU)]
        dst_x = [sb(f"dst_x{c}", [P, CT], I32) for c in range(NU)]
        lo_hotT = [sb(f"lo_hotT{c}", [P, CE]) for c in range(NU)]
        dst_hotT = [sb(f"dst_hotT{c}", [P, CE]) for c in range(NU)]
        lo_hot = sb("lo_hot", [P, R_EQ, P], BF16)
        hi_hot = sb("hi_hot", [P, R_EQ, NB], BF16)
        same = sb("same", [P, R_EQ, P], BF16)
        free_rec = [sb(f"free_rec{s}", [P, NB]) for s in range(NS)]
        picked = sb("picked", [P, R_EQ, NB])
        place = [sb(f"place{c}", [P, CT]) for c in range(NU)]
        place_i = [sb(f"place_i{c}", [P, CT], I32) for c in range(NU)]
        recs = [sb(f"recs{c}", [P, CT, REC]) for c in range(NU)]
        qk = sb("qk", [P, CT, DH])

        def pb(name, shape):
            return ctx.enter_context(nc.psum_tensor(name, shape, F32))

        ps_cnt = [pb(f"ps_cnt{s}", [P, 512]) for s in range(NS)]
        ps_feat = [pb(f"ps_feat{s}", [P, CT, KV + DH]) for s in range(2)]
        ps_eq = [pb(f"ps_eq{i}", [P, 512]) for i in range(2)]
        ps_look = [pb(f"ps_look{i}", [P, 512]) for i in range(2)]

        ones_set, dst_in = sem("ones_set"), sem("sort_dst_in")
        loaded = [sem(f"loaded{c}") for c in range(NU)]
        lo_hotT_made, dst_hotT_made = sem("lo_hotT_made"), sem("dst_hotT_made")
        dst_x_made = sem("dst_x_made")
        kv_got = [sem(f"kv_got{c}") for c in range(NU)]
        feats = sem("feats")
        kv_copied = sem("kv_copied")
        matched, masked, looked = sem("matched"), sem("masked"), sem("looked")
        hots_made = sem("hots_made")
        counted = sem("counted")
        next_ready = [sem(f"next_ready{s}") for s in range(NS)]
        placed = sem("placed")
        places_made = sem("places_made")
        dotted = sem("dotted")
        recs_made = sem("recs_made")
        units_free = sem("units_free")
        scattered = [sem(f"scattered{c}") for c in range(NU)]
        chunks_sent = sem("chunks_sent")
        NT_TURN = NU * CT
        LOADS = {False: 16 * 4, True: 16 * 2}

        def unit_chunk(it, u, s):
            return s * SC + it * HALF + u

        def tiles_of_half(u):
            return [(NS * u + s, s, j) for j in range(CT) for s in range(NS)]

        ORDER = [x for u in range(HALF) for x in tiles_of_half(u)]

        def load_loop(sp, general):
            with sp.Fori(0, TURNS) as it:
                for c, (u, s) in enumerate(UNITS):
                    chunk = unit_chunk(it, u, s)
                    sp.wait_ge(feats, NU * it + c + 1)
                    sp.dma_start(at[c][0:K_ROWS - 1, :],
                                 attr[bass.ds(chunk, 1), :, :].rearrange("a k e -> (a k) e")).then_inc(loaded[c], 16)
                    sp.dma_start(lo_b[c][:, :], spread(lo_dram, chunk)).then_inc(loaded[c], 16)
                    if not general:
                        sp.dma_start(dst_b[c][:, :], spread(dl_dram, chunk)).then_inc(loaded[c], 16)
                        w = sp.value_load(win_row[0:1, bass.ds(chunk, 1)], min_val=0, max_val=NN - P)
                        sp.dma_start(kvw[c][:, :], kv_dram[bass.ds(w, P), :]).then_inc(loaded[c], 16)

        def send_loop(pool, general):
            def turn(it, first):
                for u in range(HALF):
                    for c in range(NS * u, NS * u + NS):
                        if general:
                            pool.wait_ge(dst_x_made, NU * it + c + 1)
                            pool.sem_inc(chunks_sent, 1)
                            for j in range(CT):
                                pool.indirect_dma_start(kvg[c][:, j, :], None, kv_dram,
                                                        bass.IndirectOffsetOnAxis(dst_x[c][:, j:j + 1], 0)).then_inc(kv_got[c], 16)
                    for c in range(NS * u, NS * u + NS):
                        pool.wait_ge(recs_made, 1 + NU * it + c + 1)
                        pool.wait_ge(kv_copied, NU * it + c + 1)
                        pool.wait_ge(places_made, NU * it + c + 1)
                        pool.sem_inc(chunks_sent, 1)
                        for j in range(CT):
                            pool.indirect_dma_start(rec_dram[:, :], bass.IndirectOffsetOnAxis(place_i[c][:, j:j + 1], 0),
                                                    recs[c][:, j, :], None).then_inc(scattered[c], 16)
                        if c:
                            pool.wait_ge(scattered[c - 1], 16 * CT * it + 16 * CT)
                            pool.sem_inc(units_free, 1)
                        elif not first:
                            pool.wait_ge(scattered[NU - 1], 16 * CT * it)
                            pool.sem_inc(units_free, 1)

            pool.sem_inc(units_free, NU)
            turn(0, True)
            with pool.Fori(1, TURNS) as it:
                turn(it, False)
            pool.wait_ge(scattered[NU - 1], 16 * CT * TURNS)

        def vector_loop(dve, general):
            with dve.Fori(0, TURNS) as it:
                for u in range(HALF):
                    half = tiles_of_half(u)
                    n0 = u * len(half)
                    for s in range(NS):
                        c = NS * u + s
                        chunk = unit_chunk(it, u, s)
                        dve.wait_ge(loaded[c], LOADS[general] * it + LOADS[general])
                        dve.tensor_scalar(lo_hotT[c][:, :], lo_b[c][:, :], iota_p[:, 0:1], None,
                                          ALU.is_equal).then_inc(lo_hotT_made, 1)
                        dve.wait_ge(feats, NU * it + c + 1)
                        if general:
                            dve.tensor_copy(dst_x[c][:, :], dst_i[:, bass.ds(chunk * CT, CT)]).then_inc(dst_x_made, 1)
                        else:
                            dve.tensor_scalar(dst_hotT[c][:, :], dst_b[c][:, :], iota_p[:, 0:1], None,
                                              ALU.is_equal).then_inc(dst_hotT_made, 1)

                    def hots(k):
                        c, s, j = half[k]
                        n = NT_TURN * it + n0 + k
                        t = unit_chunk(it, u, s) * CT + j
                        slot = (n0 + k) % R_EQ
                        dve.wait_ge(counted, n + 1)
                        dve.wait_ge(placed, n + 1)
                        dve.tensor_scalar(lo_hot[:, slot, :], iota_row[:, :], lo_f[:, bass.ds(t, 1)], None, ALU.is_equal)
                        dve.tensor_scalar(hi_hot[:, slot, :], iota_row[:, 0:NB], hi_f[:, bass.ds(t, 1)], None,
                                          ALU.is_equal).then_inc(hots_made, 1)

                    def mask(k):
                        n = NT_TURN * it + n0 + k
                        dve.wait_ge(matched, n + 1)
                        dve.tensor_tensor(same[:, (n0 + k) % R_EQ, :], ps_eq[(n0 + k) % 2][:, 0:P], later[:, :],
                                          ALU.mult).then_inc(masked, 1)

                    def pick(k):
                        c, s, j = half[k]
                        n = NT_TURN * it + n0 + k
                        dve.wait_ge(looked, n + 1)
                        dve.tensor_tensor_reduce(
                            out=picked[:, (n0 + k) % R_EQ, :], in0=hi_hot[:, (n0 + k) % R_EQ, :], in1=ps_look[(n0 + k) % 2][:, 0:NB],
                            scale=1.0, scalar=0.0, op0=ALU.mult, op1=ALU.add,
                            accum_out=place[c][:, j:j + 1]).then_inc(placed, 1)

                    def logits(s):
                        c = NS * u + s
                        dve.wait_ge(kv_copied, NU * it + c + 1)
                        dve.tensor_tensor(qk[:, :, :], ps_feat[s][:, :, KV:KV + DH], recs[c][:, :, 0:DH],
                                          ALU.mult).then_inc(dotted, 1)
                        dve.wait_ge(dotted, NU * it + c + 1)
                        dve.tensor_reduce(recs[c][:, :, KV:REC], qk[:, :, :].rearrange("p j (h d) -> p j h d", h=H),
                                          AX.X, ALU.add).then_inc(recs_made, 1)

                    hots(0)
                    hots(1)
                    for k in range(len(half)):
                        mask(k)
                        if k + 2 < len(half):
                            hots(k + 2)
                        if k >= 1:
                            pick(k - 1)
                        if k in (3, 5):
                            logits((k - 3) // 2)
                    pick(len(half) - 1)
                    for s in range(NS):
                        c = NS * u + s
                        dve.wait_ge(units_free, NU * it + c + 1)
                        dve.wait_ge(placed, R_EQ + NT_TURN * it + n0 + len(half))
                        dve.tensor_copy(place_i[c][:, :], place[c][:, :]).then_inc(places_made, 1)

        def tensor_loop(pe, general):
            with pe.Fori(0, TURNS) as it:
                for u in range(HALF):
                    half = tiles_of_half(u)
                    n0 = u * len(half)

                    def features(s):
                        c = NS * u + s
                        pe.wait_ge(loaded[c], LOADS[general] * it + LOADS[general])
                        pe.wait_ge(recs_made, 1 + NU * it + NS * u)
                        if general:
                            pe.wait_ge(kv_got[c], 16 * CT * it + 16 * CT)
                        else:
                            pe.wait_ge(dst_hotT_made, NU * it + c + 1)
                        nc.tensor.matmul(ps_feat[s][:, :, :], at[c][:, :], w_attr[:, :, :], start=True, stop=False)
                        for j in range(CT):
                            hotT = ident[:, :] if general else dst_hotT[c][:, P * j:P * (j + 1)]
                            rows = kvg[c][:, j, :] if general else kvw[c][:, :]
                            last = nc.tensor.matmul(ps_feat[s][:, j, 0:KV], hotT, rows, start=False,
                                                    stop=(j == CT - 1))
                        last.then_inc(feats, 1)

                    def match(k):
                        c, s, j = half[k]
                        if k < NS:
                            pe.wait_ge(lo_hotT_made, NU * it + c + 1)
                        if n0 + k >= 2:
                            pe.wait_ge(masked, NT_TURN * it + n0 + k - 1)
                        eT = lo_hotT[c][:, P * j:P * (j + 1)]
                        nc.tensor.matmul(ps_eq[(n0 + k) % 2][:, 0:P], eT, eT, start=True, stop=True).then_inc(matched, 1)

                    def look(k):
                        c, s, j = half[k]
                        n = NT_TURN * it + n0 + k
                        slot = (n0 + k) % R_EQ
                        eT = lo_hotT[c][:, P * j:P * (j + 1)]
                        pe.wait_ge(next_ready[s], NT_TURN // NS * it + (n0 + k) // NS + 1)
                        pe.wait_ge(masked, n + 1)
                        pe.wait_ge(hots_made, n + 1)
                        pe.wait_ge(placed, R_EQ + n - 1)
                        g = ps_look[(n0 + k) % 2][:, 0:NB]
                        nc.tensor.matmul(g, eT, free_rec[s][:, :], start=True, stop=False)
                        nc.tensor.matmul(g, same[:, slot, :], hi_hot[:, slot, :], start=False, stop=True).then_inc(looked, 1)
                        nc.tensor.matmul(ps_cnt[s][:, 0:NB], lo_hot[:, slot, :], hi_hot[:, slot, :], start=False,
                                         stop=False, skip_group_check=True).then_inc(counted, 1)

                    match(0)
                    for k in range(len(half)):
                        if k + 1 < len(half):
                            match(k + 1)
                        look(k)
                        if k in (0, 2):
                            features(k // 2)

        def scalar_loop(act, general):
            with act.Fori(0, TURNS) as it:
                for u in range(HALF):
                    half = tiles_of_half(u)
                    n0 = u * len(half)
                    for k in range(len(half)):
                        c, s, j = half[k]
                        act.wait_ge(counted, R_EQ + NT_TURN * it + n0 + k + 1)
                        act.activation(free_rec[s][:, :], ps_cnt[s][:, 0:NB], ACT.Copy).then_inc(next_ready[s], 1)
                        if k in (1, 3):
                            f = k // 2
                            c = NS * u + f
                            act.wait_ge(feats, NU + NU * it + c + 1)
                            act.wait_ge(units_free, NU * it + c + 1)
                            act.activation(recs[c][:, :, 0:KV], ps_feat[f][:, :, 0:KV], ACT.Copy).then_inc(kv_copied, 1)

        def both_ways(eng, loop):
            general = eng.value_load(flag[0:1, 0:1], min_val=0, max_val=1)
            with eng.If(general < 1):
                loop(eng, False)
            with eng.Else():
                loop(eng, True)

        block = ctx.enter_context(nc.Block())

        @block.sync
        def _(sp):
            sp.dma_start(dst_i[:, :], dst_tiles).then_inc(dst_in, 16)
            sp.wait_ge(ones_set, NU)
            both_ways(sp, load_loop)

        @block.gpsimd
        def _(pool):
            both_ways(pool, send_loop)

        @block.vector
        def _(dve):
            for c in range(NU):
                dve.memset(at[c][:, :], 1.0).then_inc(ones_set, 1)
            dve.sem_inc(placed, R_EQ)
            dve.sem_inc(recs_made, 1)
            dve.wait_ge(dst_in, 16)
            both_ways(dve, vector_loop)

        @block.tensor
        def _(pe):
            pe.sem_inc(counted, R_EQ)
            pe.sem_inc(feats, NU)
            for s in range(NS):
                nc.tensor.matmul(ps_cnt[s][:, 0:NB], ident[:, :], base[:, s, :], start=True, stop=False,
                                 skip_group_check=True)
            both_ways(pe, tensor_loop)

        @block.scalar
        def _(act):
            for s in range(NS):
                act.activation(free_rec[s][:, :], base[:, s, :], ACT.Copy).then_inc(next_ready[s], 1)
            both_ways(act, scalar_loop)


def spread(table, chunk):
    return table[bass.ds(chunk, 1), :].partition_broadcast(P).rearrange("p a e -> p (a e)")


def attend_stage(nc, T, x, rec_dram, out):
    iota_f, ident, q_tab, base, deg = (T[k] for k in ("iota_f", "ident", "q_tab", "base", "deg"))
    with ExitStack() as ctx:
        def sb(name, shape, dt=F32):
            return ctx.enter_context(nc.sbuf_tensor(name, shape, dt))

        def sem(name):
            return ctx.enter_context(nc.semaphore(name))

        more_dram = nc.dram_tensor("more_dram", (NB,), I32, kind="Internal").ap()
        start_i = sb("start_i", [P, NB + 2], I32)
        most = sb("most", [NB, 1])
        more_i = sb("more_i", [NB, 1], I32)
        more = sb("more", [1, NB], I32)
        x_sb = sb("x_sb", [P, NB, DIM])
        y = sb("y", [P, NB, DIM])
        idx = [sb(f"idx{i}", [P, 1], I32) for i in range(2)]
        idx_x = sb("idx_x", [P, 1], I32)
        next_x = sb("next_x", [P, 1])
        left = sb("left", [P, 1])
        rec = [sb(f"rec{i}", [P, S0 * REC]) for i in range(2)]
        rec_x = sb("rec_x", [P, SX * REC])
        qk = sb("qk_s", [P, S0, DH])
        lg = sb("lg", [P, H, S0])
        past = sb("past", [P, S0])
        neg = sb("neg", [P, H])
        neg_x = sb("neg_x", [P, H])
        fall = sb("fall", [P, H])
        fall_e = sb("fall_e", [P, H])
        prob = sb("prob", [P, H, S0])
        den = sb("den", [P, H])
        den_x = sb("den_x", [P, H])
        msg = sb("msg", [P, S0, DIM])
        acc = sb("acc", [P, DIM])
        acc_x = sb("acc_x", [P, DIM])
        mean = sb("mean", [P, NB])
        rstd = sb("rstd", [P, NB])
        eps = sb("eps", [P, 1])
        ps_deg = ctx.enter_context(nc.psum_tensor("ps_deg", [NB, 512], F32))

        x_in, deg_up, more_made, more_out, more_in = (sem(n) for n in ("xs_in", "deg_up", "more_made", "more_out", "more_in"))
        idx_made = sem("idx_made")
        used = sem("used")
        rec_in = [sem(f"rec_in{i}") for i in range(2)]
        maxed, expd = sem("maxed"), sem("expd")
        steps = sem("block_steps")
        xi_made, xr_in, x_maxed, x_expd, x_steps = (sem(n) for n in ("xi_made", "xr_in", "x_maxed", "x_expd", "x_steps"))
        gathers = sem("gathers")
        ends, eps_set, rooted, normed, y_out = sem("ends"), sem("eps_set"), sem("rooted"), sem("normed"), sem("y_out")
        MAIN, MORE = 13, 16

        block = ctx.enter_context(nc.Block())

        @block.sync
        def _(sp):
            sp.dma_start(x_sb[:, :, :], x.rearrange("(b p) f -> p b f", p=P)).then_inc(x_in, 16)
            sp.wait_ge(more_made, 1)
            sp.dma_start(more_dram.rearrange("(b a) -> b a", a=1), more_i[:, :]).then_inc(more_out, 16)
            sp.wait_ge(more_out, 16)
            sp.dma_start(more[:, :], row_of(more_dram)).then_inc(more_in, 16)
            full = N // P
            sp.wait_ge(normed, 1)
            sp.dma_start(out[0:full * P, :].rearrange("(b p) f -> p b f", p=P), y[:, 0:full, :]).then_inc(y_out, 16)
            sp.dma_start(out[full * P:N, :], y[0:N - full * P, full, :]).then_inc(y_out, 16)
            sp.wait_ge(y_out, 32)

        @block.tensor
        def _(pe):
            nc.tensor.transpose(ps_deg[:, 0:P], deg[:, :], ident[:, :]).then_inc(deg_up, 1)

        @block.gpsimd
        def _(pool):
            for i in range(2):
                pool.wait_ge(idx_made, i + 1)
                pool.indirect_dma_start(rec[i][:, :], None, rec_dram[:, :],
                                        bass.IndirectOffsetOnAxis(idx[i][:, 0:1], 0)).then_inc(rec_in[i], 16)
            pool.wait_ge(more_in, 16)
            passes = pool.alloc_register("pool_passes")
            pool.reg_mov(passes, 0)
            with pool.Fori(0, NB // 2) as it:
                for i in range(2):
                    b = 2 * it + i
                    m = pool.value_load(more[0:1, bass.ds(b, 1)], min_val=0, max_val=EP)
                    with pool.If(m > 0):
                        with pool.Fori(0, m):
                            pool.wait_ge(xi_made, pool.snap(passes) + 1)
                            pool.sem_inc(gathers, 1)
                            pool.indirect_dma_start(rec_x[:, :], None, rec_dram[:, :],
                                                    bass.IndirectOffsetOnAxis(idx_x[:, 0:1], 0)).then_inc(xr_in, 16)
                            pool.reg_add(passes, passes, 1)
                    pool.wait_ge(idx_made, b + 3)
                    pool.wait_ge(used, b + 1)
                    pool.sem_inc(gathers, 1)
                    pool.indirect_dma_start(rec[i][:, :], None, rec_dram[:, :],
                                            bass.IndirectOffsetOnAxis(idx[i][:, 0:1], 0)).then_inc(rec_in[i], 16)
            for i in range(2):
                pool.wait_ge(rec_in[i], 16 * (NB // 2 + 1))

        @block.vector
        def _(dve):
            n = 0

            def end(ins):
                nonlocal n
                n += 1
                ins.then_inc(ends, 1)
                dve.wait_ge(ends, n)

            end(dve.memset(start_i[:, NB:NB + 2], 0))
            dve.memset(eps[:, :], 1e-5).then_inc(eps_set, 1)
            end(dve.tensor_copy(start_i[:, 0:NB], base[:, 0, :]))
            for i in range(2):
                dve.tensor_copy(idx[i][:, :], start_i[:, i:i + 1]).then_inc(idx_made, 1)
            dve.wait_ge(deg_up, 1)
            end(dve.reduce_max(most[:, :], ps_deg[:, 0:P], AX.X))
            end(dve.tensor_scalar(most[:, :], most[:, :], float(SX - 1 - S0), 0.0, ALU.add, ALU.max))
            end(dve.tensor_copy(more_i[:, :], most[:, :]))
            dve.tensor_single_scalar(more_i[:, :], more_i[:, :], int(math.log2(SX)), ALU.arith_shift_right).then_inc(more_made, 1)
            dve.wait_ge(x_in, 16)
            dve.wait_ge(more_in, 16)
            passes = dve.alloc_register("dve_passes")
            dve.reg_mov(passes, 0)

            def logits(r, slots, q, chain):
                v = r[:, :].rearrange("p (s f) -> p s f", f=REC)
                by_slot = lg[:, :, 0:slots].rearrange("p h s -> p s h")
                chain(dve.tensor_tensor(qk[:, 0:slots, :], v[:, :, 0:DH], q.broadcast_to((P, slots, DH)), ALU.mult))
                chain(dve.tensor_reduce(by_slot, qk[:, 0:slots, :].rearrange("p s (h d) -> p s h d", h=H), AX.X, ALU.add))
                chain(dve.tensor_tensor(by_slot, by_slot, v[:, :, KV:REC], ALU.add))
                chain(dve.tensor_tensor(lg[:, :, 0:slots], lg[:, :, 0:slots],
                                        past[:, 0:slots].unsqueeze(1).broadcast_to((P, H, slots)), ALU.add))

            def messages(r, slots):
                v = r[:, :].rearrange("p (s f) -> p s f", f=REC)
                return dve.tensor_tensor(
                    msg[:, 0:slots, :].rearrange("p s (h d) -> p s h d", h=H),
                    v[:, :, DH:KV].rearrange("p s (h d) -> p s h d", h=H),
                    prob[:, :, 0:slots].rearrange("p h s -> p s h").unsqueeze(3).broadcast_to((P, slots, H, VD)), ALU.mult)

            def summed(slots, total):
                return dve.tensor_reduce(total[:, :], msg[:, 0:slots, :].rearrange("p s f -> p f s"), AX.X, ALU.add)

            def by_head(t):
                return t.rearrange("p (h d) -> p h d", h=H)

            with dve.Fori(0, NB // 2) as it:
                for i in range(2):
                    b = 2 * it + i
                    k = 0

                    def chain(ins):
                        nonlocal k
                        k += 1
                        ins.then_inc(steps, 1)
                        dve.wait_ge(steps, MAIN * b + k)

                    dve.wait_ge(rec_in[i], 16 * it + 16)
                    dve.tensor_copy(idx[i][:, :], start_i[:, bass.ds(b + 2, 1)]).then_inc(idx_made, 1)
                    chain(dve.tensor_scalar(past[:, :], iota_f[:, 0:S0], deg[:, bass.ds(b, 1)], -BIG, ALU.is_ge, ALU.mult))
                    logits(rec[i], S0, q_tab[:, bass.ds(b, 1), :], chain)
                    chain(dve.tensor_reduce(neg[:, :], lg[:, :, :], AX.X, ALU.max, negate=True))
                    dve.tensor_single_scalar(neg[:, :], neg[:, :], BIG / 2, ALU.min).then_inc(maxed, 1)
                    chain(dve.tensor_single_scalar(left[:, :], deg[:, bass.ds(b, 1)], -float(S0), ALU.add))
                    chain(dve.tensor_scalar(next_x[:, :], base[:, 0, bass.ds(b, 1)], float(S0), float(EP), ALU.add, ALU.min))
                    dve.wait_ge(expd, b + 1)
                    messages(rec[i], S0).then_inc(used, 1)
                    dve.wait_ge(used, b + 1)
                    chain(summed(S0, acc))
                    m = dve.value_load(more[0:1, bass.ds(b, 1)], min_val=0, max_val=EP)
                    with dve.If(m > 0):
                        with dve.Fori(0, m):
                            done = dve.snap(passes)
                            kx = 0

                            def xchain(ins):
                                nonlocal kx
                                kx += 1
                                ins.then_inc(x_steps, 1)
                                dve.wait_ge(x_steps, MORE * done + kx)

                            dve.tensor_copy(idx_x[:, :], next_x[:, :]).then_inc(xi_made, 1)
                            xchain(dve.tensor_scalar(past[:, 0:SX], iota_f[:, 0:SX], left[:, 0:1], -BIG, ALU.is_ge, ALU.mult))
                            xchain(dve.tensor_scalar(next_x[:, :], next_x[:, :], float(SX), float(EP), ALU.add, ALU.min))
                            xchain(dve.tensor_single_scalar(left[:, :], left[:, :], -float(SX), ALU.add))
                            dve.wait_ge(xr_in, 16 * done + 16)
                            logits(rec_x, SX, q_tab[:, bass.ds(b, 1), :], xchain)
                            xchain(dve.tensor_reduce(neg_x[:, :], lg[:, :, 0:SX], AX.X, ALU.max, negate=True))
                            xchain(dve.tensor_tensor(neg_x[:, :], neg_x[:, :], neg[:, :], ALU.min))
                            dve.tensor_tensor(fall[:, :], neg_x[:, :], neg[:, :], ALU.subtract).then_inc(x_maxed, 1)
                            dve.wait_ge(x_maxed, done + 1)
                            xchain(dve.tensor_copy(neg[:, :], neg_x[:, :]))
                            dve.wait_ge(x_expd, done + 1)
                            xchain(dve.tensor_tensor(den[:, :], den[:, :], fall_e[:, :], ALU.mult))
                            xchain(dve.tensor_tensor(den[:, :], den[:, :], den_x[:, :], ALU.add))
                            xchain(dve.tensor_tensor(by_head(acc[:, :]), by_head(acc[:, :]),
                                                     fall_e[:, :].unsqueeze(2).broadcast_to((P, H, VD)), ALU.mult))
                            xchain(messages(rec_x, SX))
                            xchain(summed(SX, acc_x))
                            xchain(dve.tensor_tensor(acc[:, :], acc[:, :], acc_x[:, :], ALU.add))
                            assert kx == MORE, kx
                            dve.reg_add(passes, passes, 1)
                    chain(dve.tensor_single_scalar(den[:, :], den[:, :], 1e-16, ALU.add))
                    chain(dve.reciprocal(den[:, :], den[:, :]))
                    chain(dve.tensor_tensor(by_head(acc[:, :]), by_head(acc[:, :]),
                                            den[:, :].unsqueeze(2).broadcast_to((P, H, VD)), ALU.mult))
                    chain(dve.tensor_tensor(y[:, bass.ds(b, 1), :].rearrange("p a f -> p (a f)"), acc[:, :],
                                            x_sb[:, bass.ds(b, 1), :].rearrange("p a f -> p (a f)"), ALU.add))
                    assert k == MAIN, k
            end(dve.tensor_reduce(mean[:, :], y[:, :, :], AX.X, ALU.add))
            end(dve.tensor_single_scalar(mean[:, :], mean[:, :], 1.0 / DIM, ALU.mult))
            end(dve.tensor_tensor(y[:, :, :], y[:, :, :], mean[:, :].unsqueeze(2).broadcast_to((P, NB, DIM)), ALU.subtract))
            end(dve.tensor_tensor(x_sb[:, :, :], y[:, :, :], y[:, :, :], ALU.mult))
            end(dve.tensor_reduce(mean[:, :], x_sb[:, :, :], AX.X, ALU.add))
            dve.wait_ge(rooted, 1)
            end(dve.reciprocal(rstd[:, :], rstd[:, :]))
            dve.tensor_tensor(y[:, :, :], y[:, :, :], rstd[:, :].unsqueeze(2).broadcast_to((P, NB, DIM)),
                              ALU.mult).then_inc(normed, 1)
            assert n == 5 + 5 + 1, n

        @block.scalar
        def _(act):
            def exps(slots, negated, total, done):
                for h in range(H):
                    last = act.activation(prob[:, h, 0:slots], lg[:, h, 0:slots], ACT.Exp, bias=negated[:, h:h + 1],
                                          accum_out=total[:, h:h + 1])
                last.then_inc(done, 1)

            act.wait_ge(more_in, 16)
            passes = act.alloc_register("act_passes")
            act.reg_mov(passes, 0)
            with act.Fori(0, NB) as b:
                act.wait_ge(maxed, b + 1)
                exps(S0, neg, den, expd)
                m = act.value_load(more[0:1, bass.ds(b, 1)], min_val=0, max_val=EP)
                with act.If(m > 0):
                    with act.Fori(0, m):
                        act.wait_ge(x_maxed, act.snap(passes) + 1)
                        act.activation(fall_e[:, :], fall[:, :], ACT.Exp)
                        exps(SX, neg_x, den_x, x_expd)
                        act.reg_add(passes, passes, 1)
            act.wait_ge(eps_set, 1)
            act.wait_ge(ends, 10)
            act.activation(rstd[:, :], mean[:, :], ACT.Sqrt, bias=eps[:, 0:1], scale=1.0 / DIM).then_inc(rooted, 1)


def kernel(x, src, dst, edge_attr_18, L0_gnn_qkv_w, L0_gnn_qkv_b, L0_gnn_k_rpe_w, L0_gnn_k_rpe_b,
           L0_gnn_q_rpe_w, L0_gnn_q_rpe_b, L0_gnn_v_rpe_w, L0_gnn_v_rpe_b):
    import concourse.bacc as bacc
    from concourse.bass_utils import run_bass_kernel_spmd

    x, src, dst, attr = (np.asarray(a) for a in (x, src, dst, edge_attr_18))
    pad = (N + np.arange(EP - E) % (NN - N)).astype(np.int32)
    src = np.concatenate([src, pad])
    dst = np.concatenate([dst, pad])
    attr = np.concatenate([attr, np.zeros((EP - E, ATTR), attr.dtype)])
    x = np.concatenate([x, np.zeros((NN - N, DIM), x.dtype)])
    arrays = {
        "x": x,
        "xT": np.ascontiguousarray(x.T),
        "src_lin": src,
        "src_tiles": np.ascontiguousarray(src.reshape(NT, P).T),
        "dst_lin": dst,
        "dst_tiles": np.ascontiguousarray(dst.reshape(NT, P).T),
        "attr": np.ascontiguousarray(attr.reshape(NCH, CT, P, ATTR).transpose(0, 1, 3, 2)).reshape(NCH, CT * ATTR, P),
        "qkv_w": L0_gnn_qkv_w, "qkv_b": L0_gnn_qkv_b, "k_rpe_w": L0_gnn_k_rpe_w, "k_rpe_b": L0_gnn_k_rpe_b,
        "q_rpe_w": L0_gnn_q_rpe_w, "q_rpe_b": L0_gnn_q_rpe_b, "v_rpe_w": L0_gnn_v_rpe_w, "v_rpe_b": L0_gnn_v_rpe_b,
    }
    nc = bacc.Bacc("TRN2", target_bir_lowering=False, num_devices=1)
    feed, args = {}, []
    for name, a in arrays.items():
        a = np.ascontiguousarray(a)
        feed[f"in_{name}"] = a
        args.append(nc.dram_tensor(f"in_{name}", a.shape, mybir.dt.from_np(a.dtype), kind="ExternalInput").ap())
    args.append(nc.dram_tensor("out_y", (N, DIM), F32, kind="ExternalOutput").ap())
    gnn_kernel(nc, *args)
    r = run_bass_kernel_spmd(nc, [feed], core_ids=[0])
    return r.results[0]["out_y"]
```

```python
import math
from contextlib import ExitStack

import numpy as np
import concourse.bass as bass
from concourse import mybir

F32 = mybir.dt.float32
BF16 = mybir.dt.bfloat16
I32 = mybir.dt.int32
ALU = mybir.AluOpType
ACT = mybir.ActivationFunctionType
AX = mybir.AxisListType

P = 128
N, E = 12500, 412500
DIM, H, D = 64, 4, 8
DH, VD = H * D, DIM // H
ATTR = 18
NB = math.ceil(N / P)
NN = NB * P
CT = 4
CE = CT * P
NS = 2
HALF = 2
NCH = math.ceil(E / (CE * NS * HALF)) * NS * HALF
EP = NCH * CE
NT = NCH * CT
SC = NCH // NS
TURNS = SC // HALF
TT = NS * HALF * CT
KV = DH + DIM
REC = KV + H
WP = 101
WG = NCH // WP
K_ROWS = CT * ATTR + 1
BIG = 1.0e30
S0 = 56
SX = 16
RROWS = EP + S0 + SX
XG = 7
assert WP * WG == NCH and NCH % (NS * HALF) == 0 and NB % (2 * XG) == 0 and NT % (NS * 16) == 0


def row_of(v):
    return v.rearrange("(a n) -> a n", a=1)


def gnn_kernel(nc, x, xT, src_lin, src_tiles, dst_lin, dst_tiles, attr, qkv_w, qkv_b, k_rpe_w, k_rpe_b,
               q_rpe_w, q_rpe_b, v_rpe_w, v_rpe_b, out):
    lo_dram = nc.dram_tensor("lo_dram", (NCH, CE), BF16, kind="Internal").ap()
    dl_dram = nc.dram_tensor("dl_dram", (NCH, CE), BF16, kind="Internal").ap()
    win_dram = nc.dram_tensor("win_dram", (NCH,), I32, kind="Internal").ap()
    over_dram = nc.dram_tensor("over_dram", (NCH,), F32, kind="Internal").ap()
    kv_dram = nc.dram_tensor("kv_dram", (NN, KV), F32, kind="Internal").ap()
    rec_dram = nc.dram_tensor("rec_dram", (RROWS, REC), F32, kind="Internal").ap()

    with ExitStack() as keep:
        def kept(name, shape, dt=F32):
            return keep.enter_context(nc.sbuf_tensor(name, shape, dt))

        T = dict(
            iota_row=kept("iota_row", [P, P], BF16),
            iota_f=kept("iota_f", [P, P]),
            iota_p=kept("iota_p", [P, 1]),
            ident=kept("ident", [P, P]),
            later=kept("later", [P, P]),
            lo_f=kept("lo_f", [P, NT]),
            hi_f=kept("hi_f", [P, NT]),
            q_tab=kept("q_tab", [P, NB, DH]),
            base=kept("base", [P, NS, NB]),
            deg=kept("deg", [P, NB]),
            w_attr=kept("w_attr", [P, CT, KV + DH]),
            win_row=kept("win_row", [1, NCH], I32),
            flag=kept("flag", [1, 1], I32),
        )
        tables_stage(nc, T, xT, src_lin, src_tiles, dst_lin, qkv_w, qkv_b, k_rpe_w, k_rpe_b,
                     q_rpe_w, q_rpe_b, v_rpe_w, v_rpe_b, lo_dram, dl_dram, win_dram, over_dram, kv_dram,
                     rec_dram)
        sort_stage(nc, T, attr, dst_tiles, lo_dram, dl_dram, kv_dram, rec_dram)
        attend_stage(nc, T, x, rec_dram, out)


def tables_stage(nc, T, xT, src_lin, src_tiles, dst_lin, qkv_w, qkv_b, k_rpe_w, k_rpe_b,
                 q_rpe_w, q_rpe_b, v_rpe_w, v_rpe_b, lo_dram, dl_dram, win_dram, over_dram, kv_dram,
                 rec_dram):
    iota_row, iota_f, iota_p, ident, later = (T[k] for k in ("iota_row", "iota_f", "iota_p", "ident", "later"))
    lo_f, hi_f, q_tab, base, deg, w_attr = (T[k] for k in ("lo_f", "hi_f", "q_tab", "base", "deg", "w_attr"))
    win_row, flag = T["win_row"], T["flag"]
    GROUP = 8
    PER_TURN = 2 * GROUP
    with ExitStack() as ctx:
        def sb(name, shape, dt=F32):
            return ctx.enter_context(nc.sbuf_tensor(name, shape, dt))

        def sem(name):
            return ctx.enter_context(nc.semaphore(name))

        iota_i = sb("iota_i", [P, P], I32)
        iota_pi = sb("iota_pi", [P, 1], I32)
        src_i = sb("src_i", [P, NT], I32)
        dig_i = sb("dig_i", [P, NT], I32)
        srcl_i = sb("srcl_i", [P, NT], I32)
        lo_lin = sb("lo_lin", [P, NT], BF16)
        dst_l = sb("dst_l", [WP, WG, CE], I32)
        dst_loc = sb("dst_loc", [WP, WG, CE], BF16)
        win_f = sb("win_f", [WP, WG])
        win_i = sb("win_i", [WP, WG], I32)
        over = sb("over", [WP, WG])
        over_row = sb("over_row", [1, NCH])
        flag_f = sb("flag_f", [1, 1])
        ones = sb("ones", [P, NB])
        incl = sb("incl", [P, NB])
        row_base = sb("row_base", [P, 1])
        h_lo = [sb(f"h_lo{i}", [P, GROUP, P], BF16) for i in range(2)]
        h_hi = [sb(f"h_hi{i}", [P, GROUP, NB], BF16) for i in range(2)]
        zeros = sb("zeros", [P, NS * NB], BF16)
        w_qkv = sb("w_qkv", [DIM + 1, 2 * DH + DIM])
        xt = [sb(f"xt{i}", [DIM + 1, XG * P]) for i in range(2)]
        kvt = sb("kvt", [P, NB, KV])
        tail = sb("tail", [S0 + SX, REC])
        ps_hist = ctx.enter_context(nc.psum_tensor("ps_hist", [P, NS, 256], F32))
        ps_row = ctx.enter_context(nc.psum_tensor("ps_row", [P, 512], F32))
        ps_x = [ctx.enter_context(nc.psum_tensor(f"ps_x{i}", [P, 8, P], F32)) for i in range(2)]

        src_in, srcl_in, dst_in = sem("src_in"), sem("srcl_in"), sem("dst_in")
        w_zero, w_in, x_ones = sem("w_zero"), sem("w_in"), sem("x_ones")
        iotas, consts, diag = sem("iotas"), sem("consts"), sem("diag")
        steps = sem("steps")
        lo_made, lo_out = sem("lo_made"), sem("lo_out")
        loc_made, loc_out = sem("loc_made"), sem("loc_out")
        win_made, win_out, win_in, flag_made = sem("win_made"), sem("win_out"), sem("win_in"), sem("flag_made")
        hot, tallied = sem("hot"), sem("tallied")
        sums_made, rows_summed = sem("sums_made"), sem("rows_summed")
        tail_zero, tail_out = sem("tail_zero"), sem("tail_out")
        x_in = [sem(f"x_in{i}") for i in range(2)]
        x_done, q_read = sem("x_done"), sem("q_read")
        kv_read = sem("kv_read")
        kv_out = sem("kv_out")
        n_w = 2 + 6 * CT

        block = ctx.enter_context(nc.Block())

        @block.sync
        def _(sp):
            sp.dma_start(src_i[:, :], src_tiles).then_inc(src_in, 16)
            sp.dma_start(srcl_i[:, :], src_lin.rearrange("(p t) -> p t", p=P)).then_inc(srcl_in, 16)
            sp.dma_start(dst_l[:, :, :], dst_lin.rearrange("(p g e) -> p g e", p=WP, g=WG)).then_inc(dst_in, 16)
            sp.dma_start(w_qkv[0:DIM, :], qkv_w).then_inc(w_in, 16)
            sp.dma_start(w_qkv[DIM:DIM + 1, :], row_of(qkv_b)).then_inc(w_in, 16)
            sp.wait_ge(w_zero, 1)
            for j in range(CT):
                for c, w, b in ((0, k_rpe_w, k_rpe_b), (DH, v_rpe_w, v_rpe_b), (KV, q_rpe_w, q_rpe_b)):
                    n = w.shape[1]
                    sp.dma_start(w_attr[ATTR * j:ATTR * (j + 1), j, c:c + n], w).then_inc(w_in, 16)
                    sp.dma_start(w_attr[K_ROWS - 1:K_ROWS, j, c:c + n], row_of(b)).then_inc(w_in, 16)
            sp.wait_ge(x_ones, 2)
            with sp.Fori(0, NB // (2 * XG)) as it:
                for i in range(2):
                    sp.wait_ge(x_done, 2 * it + i + 1)
                    sp.dma_start(xt[i][0:DIM, :], xT[:, bass.ds((2 * it + i) * XG * P, XG * P)]).then_inc(x_in[i], 16)
            sp.wait_ge(lo_made, 1)
            sp.dma_start(lo_dram.rearrange("c e -> (c e)").rearrange("(p t) -> p t", p=P), lo_lin[:, :]).then_inc(lo_out, 16)
            sp.wait_ge(loc_made, WG)
            sp.dma_start(dl_dram.rearrange("(p g) e -> p g e", p=WP), dst_loc[:, :, :]).then_inc(loc_out, 16)
            sp.wait_ge(win_made, 2)
            sp.dma_start(win_dram.rearrange("(p g) -> p g", p=WP), win_i[:, :]).then_inc(win_out, 16)
            sp.dma_start(over_dram.rearrange("(p g) -> p g", p=WP), over[:, :]).then_inc(win_out, 16)
            sp.wait_ge(win_out, 32)
            sp.dma_start(win_row[:, :], row_of(win_dram)).then_inc(win_in, 16)
            sp.dma_start(over_row[:, :], row_of(over_dram)).then_inc(win_in, 16)
            sp.wait_ge(kv_read, NB // XG)
            sp.dma_start(kv_dram.rearrange("(b p) f -> p b f", p=P), kvt[:, :, :]).then_inc(kv_out, 16)
            sp.wait_ge(kv_out, 16)
            sp.wait_ge(tail_zero, 1)
            sp.dma_start(rec_dram[EP:RROWS, :], tail[:, :]).then_inc(tail_out, 16)
            sp.wait_ge(tail_out, 16)
            sp.wait_ge(lo_out, 16)
            sp.wait_ge(loc_out, 16)
            sp.wait_ge(win_in, 32)
            sp.wait_ge(w_in, 16 * n_w)

        @block.gpsimd
        def _(pool):
            pool.iota(iota_i[:, :], pattern=[[1, P]], base=0, channel_multiplier=0).then_inc(iotas, 1)
            pool.iota(iota_pi[:, :], pattern=[[0, 1]], base=0, channel_multiplier=1).then_inc(iotas, 1)
            pool.memset(ident[:, :], 0.0).then_inc(diag, 1)
            pool.memset(later[:, :], 1.0).then_inc(diag, 1)
            pool.wait_ge(diag, 2)
            pool.affine_select(out=ident[:, :], in_=ident[:, :], compare_op=ALU.not_equal, fill=1.0,
                               base=0, pattern=[[-1, P]], channel_multiplier=1).then_inc(diag, 1)
            pool.affine_select(out=later[:, :], in_=later[:, :], compare_op=ALU.is_gt, fill=0.0,
                               base=0, pattern=[[1, P]], channel_multiplier=-1).then_inc(diag, 1)
            pool.wait_ge(diag, 4)

        @block.vector
        def _(dve):
            dve.memset(w_attr[:, :, :], 0.0).then_inc(w_zero, 1)
            dve.memset(xt[0][DIM:DIM + 1, :], 1.0).then_inc(x_ones, 1)
            dve.memset(xt[1][DIM:DIM + 1, :], 1.0).then_inc(x_ones, 1)
            dve.memset(tail[:, :], 0.0).then_inc(tail_zero, 1)
            dve.memset(ones[:, :], 1.0).then_inc(consts, 1)
            dve.memset(zeros[:, :], 0.0).then_inc(consts, 1)
            dve.wait_ge(iotas, 2)
            dve.tensor_copy(iota_row[:, :], iota_i[:, :]).then_inc(consts, 1)
            dve.tensor_copy(iota_f[:, :], iota_i[:, :]).then_inc(consts, 1)
            dve.tensor_copy(iota_p[:, :], iota_pi[:, :]).then_inc(consts, 1)
            n = 0

            def step(ins):
                nonlocal n
                n += 1
                ins.then_inc(steps, 1)
                dve.wait_ge(steps, n)

            dve.wait_ge(src_in, 16)
            step(dve.tensor_single_scalar(dig_i[:, :], src_i[:, :], P - 1, ALU.bitwise_and))
            step(dve.tensor_copy(lo_f[:, :], dig_i[:, :]))
            step(dve.tensor_single_scalar(dig_i[:, :], src_i[:, :], 7, ALU.arith_shift_right))
            step(dve.tensor_copy(hi_f[:, :], dig_i[:, :]))
            dve.wait_ge(consts, 5)
            dve.wait_ge(srcl_in, 16)
            step(dve.tensor_single_scalar(dig_i[:, :], srcl_i[:, :], P - 1, ALU.bitwise_and))
            dve.tensor_copy(lo_lin[:, :], dig_i[:, :]).then_inc(lo_made, 1)
            dve.wait_ge(dst_in, 16)
            step(dve.tensor_reduce(win_f[:, :], dst_l[:, :, :], AX.X, ALU.min))
            step(dve.tensor_single_scalar(win_f[:, :], win_f[:, :], float(NN - P), ALU.min))
            step(dve.tensor_reduce(over[:, :], dst_l[:, :, :], AX.X, ALU.max))
            dve.tensor_copy(win_i[:, :], win_f[:, :]).then_inc(win_made, 1)
            dve.tensor_sub(over[:, :], over[:, :], win_f[:, :]).then_inc(win_made, 1)
            for g in range(WG):
                dve.tensor_scalar(dst_loc[:, g, :], dst_l[:, g, :], win_f[:, g:g + 1], None,
                                  ALU.subtract).then_inc(loc_made, 1)
            with dve.Fori(0, NT // PER_TURN) as it:
                for i in range(2):
                    dve.wait_ge(tallied, 2 * it + i + 1)
                    t = PER_TURN * it + GROUP * i
                    dve.tensor_tensor(h_lo[i][:, :, :], iota_row[:, :].unsqueeze(1).broadcast_to((P, GROUP, P)),
                                      lo_f[:, bass.ds(t, GROUP)].unsqueeze(2).broadcast_to((P, GROUP, P)), ALU.is_equal)
                    dve.tensor_tensor(h_hi[i][:, :, :], iota_row[:, 0:NB].unsqueeze(1).broadcast_to((P, GROUP, NB)),
                                      hi_f[:, bass.ds(t, GROUP)].unsqueeze(2).broadcast_to((P, GROUP, NB)),
                                      ALU.is_equal).then_inc(hot, 1)
            dve.wait_ge(win_in, 32)
            step(dve.reduce_max(flag_f[:, :], over_row[:, :], AX.X))
            step(dve.tensor_single_scalar(flag_f[:, :], flag_f[:, :], float(P), ALU.is_ge))
            dve.tensor_copy(flag[:, :], flag_f[:, :]).then_inc(flag_made, 1)
            dve.wait_ge(tallied, 2 + NT // GROUP)
            step(dve.tensor_copy(base[:, :, :], ps_hist[:, :, 0:NB]))
            step(dve.tensor_add(deg[:, :], base[:, 0, :], base[:, 1, :]))
            step(dve.tensor_tensor_scan(incl[:, :], ones[:, :], deg[:, :], 0.0, ALU.mult, ALU.add))
            sums = dve.tensor_sub(incl[:, 0:NB - 1], incl[:, 0:NB - 1], deg[:, 0:NB - 1])
            sums.then_inc(sums_made, 1)
            dve.wait_ge(sums_made, 1)
            dve.wait_ge(rows_summed, 1)
            step(dve.tensor_copy(row_base[:, :], ps_row[:, 0:1]))
            step(dve.tensor_sub(incl[:, NB - 1:NB], incl[:, NB - 1:NB], deg[:, NB - 1:NB]))
            step(dve.tensor_scalar(incl[:, :], incl[:, :], row_base[:, 0:1], None, ALU.add))
            step(dve.tensor_add(base[:, 1, :], base[:, 0, :], incl[:, :]))
            step(dve.tensor_copy(base[:, 0, :], incl[:, :]))
            dve.wait_ge(loc_made, WG)
            dve.wait_ge(flag_made, 1)
            dve.wait_ge(lo_made, 1)

        @block.tensor
        def _(pe):
            pe.sem_inc(x_done, 2)
            pe.sem_inc(tallied, 2)
            pe.wait_ge(w_in, 16 * n_w)
            with pe.Fori(0, NB // (2 * XG)) as it:
                for i in range(2):
                    pe.wait_ge(x_in[i], 16 * it + 16)
                    pe.wait_ge(q_read, 2 * it + i + 1)
                    for b in range(XG):
                        last = nc.tensor.matmul(ps_x[i][:, b, :], xt[i][:, b * P:(b + 1) * P], w_qkv[:, :],
                                                start=True, stop=True)
                    last.then_inc(x_done, 1)
            pe.wait_ge(consts, 5)
            nc.tensor.matmul(ps_hist[:, :, 0:NB], zeros[:, 0:P], zeros[:, :].rearrange("p (s b) -> p s b", s=NS),
                             start=True, stop=False, skip_group_check=True)
            groups = NT // NS // GROUP
            for s in range(NS):
                with pe.Fori(0, groups // 2) as it:
                    for i in range(2):
                        pe.wait_ge(hot, groups * s + 2 * it + i + 1)
                        for k in range(GROUP):
                            last = nc.tensor.matmul(ps_hist[:, s, 0:NB], h_lo[i][:, k, :], h_hi[i][:, k, :],
                                                    start=False, stop=False, skip_group_check=True)
                        last.then_inc(tallied, 1)
            pe.wait_ge(sums_made, 1)
            pe.wait_ge(diag, 4)
            nc.tensor.matmul(ps_row[:, 0:1], later[:, :], incl[:, NB - 1:NB], start=True,
                             stop=True).then_inc(rows_summed, 1)

        @block.scalar
        def _(act):
            act.sem_inc(q_read, 2)
            with act.Fori(0, NB // (2 * XG)) as it:
                for i in range(2):
                    act.wait_ge(x_done, 2 + 2 * it + i + 1)
                    act.activation(kvt[:, bass.ds((2 * it + i) * XG, XG), :], ps_x[i][:, 0:XG, DH:DH + KV], ACT.Copy).then_inc(kv_read, 1)
                    act.activation(q_tab[:, bass.ds((2 * it + i) * XG, XG), :], ps_x[i][:, 0:XG, 0:DH], ACT.Copy,
                                   scale=float(D) ** -0.5).then_inc(q_read, 1)


def sort_stage(nc, T, attr, dst_tiles, lo_dram, dl_dram, kv_dram, rec_dram):
    iota_row, iota_f, iota_p, ident, later = (T[k] for k in ("iota_row", "iota_f", "iota_p", "ident", "later"))
    lo_f, hi_f, base, w_attr, win_row, flag = (T[k] for k in ("lo_f", "hi_f", "base", "w_attr", "win_row", "flag"))
    UNITS = [(u, s) for u in range(HALF) for s in range(NS)]
    with ExitStack() as ctx:
        def sb(name, shape, dt=F32):
            return ctx.enter_context(nc.sbuf_tensor(name, shape, dt))

        def sem(name):
            return ctx.enter_context(nc.semaphore(name))

        NU = len(UNITS)
        dst_i = sb("dst_i", [P, NT], I32)
        lo_b = [sb(f"lo_b{c}", [P, CE], BF16) for c in range(NU)]
        dst_b = [sb(f"dst_b{c}", [P, CE], BF16) for c in range(NU)]
        at = [sb(f"at{c}", [P, P]) for c in range(NU)]
        kvw = [sb(f"kvw{c}", [P, KV]) for c in range(NU)]
        kvg = [sb(f"kvg{c}", [P, CT, KV]) for c in range(NU)]
        dst_x = [sb(f"dst_x{c}", [P, CT], I32) for c in range(NU)]
        lo_hotT = [sb(f"lo_hotT{c}", [P, CE]) for c in range(NU)]
        dst_hotT = [sb(f"dst_hotT{c}", [P, CE]) for c in range(NU)]
        lo_hot = [sb(f"lo_hot{c}", [P, CT, P], BF16) for c in range(NU)]
        hi_hot = [sb(f"hi_hot{c}", [P, CT, NB], BF16) for c in range(NU)]
        same = [sb(f"same{i}", [P, NS, P], BF16) for i in range(2)]
        free_rec = [sb(f"free_rec{s}", [P, NB]) for s in range(NS)]
        picked = [[sb(f"picked{i}{s}", [P, NB]) for s in range(NS)] for i in range(2)]
        place = [sb(f"place{c}", [P, CT]) for c in range(NU)]
        place_i = [sb(f"place_i{c}", [P, CT], I32) for c in range(NU)]
        recs = [sb(f"recs{c}", [P, CT, REC]) for c in range(NU)]
        qk = [sb(f"qk{s}", [P, CT, DH]) for s in range(NS)]
        not_later = sb("not_later", [P, NS, P], BF16)
        ident_b = sb("ident_b", [P, P], BF16)

        def pb(name, shape):
            return ctx.enter_context(nc.psum_tensor(name, shape, F32))

        ps_cnt = [pb(f"ps_cnt{s}", [P, 512]) for s in range(NS)]
        ps_feat = [pb(f"ps_feat{s}", [P, CT, KV + DH]) for s in range(2)]
        ps_eq = [pb(f"ps_eq{i}", [P, 512]) for i in range(2)]
        ps_look = [pb(f"ps_look{i}", [P, 512]) for i in range(2)]

        consts, ones_set, dst_in = sem("sort_consts"), sem("ones_set"), sem("sort_dst_in")
        loaded = [sem(f"loaded{c}") for c in range(NU)]
        lo_hotT_made, dst_hotT_made, hots_made = sem("lo_hotT_made"), sem("dst_hotT_made"), sem("hots_made")
        dst_x_made = sem("dst_x_made")
        kv_got = [sem(f"kv_got{c}") for c in range(NU)]
        feats = sem("feats")
        kv_copied, dotted = sem("kv_copied"), sem("dotted")
        recs_made = sem("recs_made")
        units_free = sem("units_free")
        matched, looked = sem("matched"), sem("looked")
        masked = sem("masked")
        placed = sem("placed")
        counted = [sem(f"counted{s}") for s in range(NS)]
        next_ready = [sem(f"next_ready{s}") for s in range(NS)]
        places_made = sem("places_made")
        scattered = [sem(f"scattered{c}") for c in range(NU)]
        chunks_sent = sem("chunks_sent")
        LOADS = {False: 16 * 4, True: 16 * 2}

        def unit_chunk(it, u, s):
            return s * SC + it * HALF + u

        def turns(eng, turn):
            with eng.Fori(0, TURNS - 1) as it:
                turn(it, False)
            turn(TURNS - 1, True)

        def load_loop(sp, general):
            with sp.Fori(0, TURNS) as it:
                for c, (u, s) in enumerate(UNITS):
                    chunk = unit_chunk(it, u, s)
                    sp.wait_ge(feats, NU * it + c + 1)
                    sp.dma_start(at[c][0:K_ROWS - 1, :],
                                 attr[bass.ds(chunk, 1), :, :].rearrange("a k e -> (a k) e")).then_inc(loaded[c], 16)
                    sp.dma_start(lo_b[c][:, :], spread(lo_dram, chunk)).then_inc(loaded[c], 16)
                    if not general:
                        sp.dma_start(dst_b[c][:, :], spread(dl_dram, chunk)).then_inc(loaded[c], 16)
                        w = sp.value_load(win_row[0:1, bass.ds(chunk, 1)], min_val=0, max_val=NN - P)
                        sp.dma_start(kvw[c][:, :], kv_dram[bass.ds(w, P), :]).then_inc(loaded[c], 16)

        def send_loop(pool, general):
            def turn(it, first):
                for u in range(HALF):
                    for c in range(NS * u, NS * u + NS):
                        if general:
                            pool.wait_ge(dst_x_made, NU * it + c + 1)
                            pool.sem_inc(chunks_sent, 1)
                            for j in range(CT):
                                pool.indirect_dma_start(kvg[c][:, j, :], None, kv_dram,
                                                        bass.IndirectOffsetOnAxis(dst_x[c][:, j:j + 1], 0)).then_inc(kv_got[c], 16)
                    for c in range(NS * u, NS * u + NS):
                        pool.wait_ge(recs_made, NS + NU * it + c + 1)
                        pool.wait_ge(kv_copied, NU * it + c + 1)
                        pool.wait_ge(places_made, NU * it + c + 1)
                        pool.sem_inc(chunks_sent, 1)
                        for j in range(CT):
                            pool.indirect_dma_start(rec_dram[:, :], bass.IndirectOffsetOnAxis(place_i[c][:, j:j + 1], 0),
                                                    recs[c][:, j, :], None).then_inc(scattered[c], 16)
                        if c:
                            pool.wait_ge(scattered[c - 1], 16 * CT * it + 16 * CT)
                            pool.sem_inc(units_free, 1)
                        elif not first:
                            pool.wait_ge(scattered[NU - 1], 16 * CT * it)
                            pool.sem_inc(units_free, 1)

            pool.sem_inc(units_free, NU)
            turn(0, True)
            with pool.Fori(1, TURNS) as it:
                turn(it, False)
            pool.wait_ge(scattered[NU - 1], 16 * CT * TURNS)

        def vector_loop(dve, general):
            def columns(it, u, s):
                c = NS * u + s
                half = HALF * it + u
                dve.wait_ge(loaded[c], LOADS[general] * it + LOADS[general])
                if not (isinstance(half, int) and half == 0):
                    dve.wait_ge(counted[s], 1 + CT * (half - 1))
                dve.tensor_scalar(lo_hotT[c][:, :], lo_b[c][:, :], iota_p[:, 0:1], None, ALU.is_equal).then_inc(lo_hotT_made, 1)
                dve.wait_ge(feats, NU * it + c + 1)
                if general:
                    dve.tensor_copy(dst_x[c][:, :], dst_i[:, bass.ds(unit_chunk(it, u, s) * CT, CT)]).then_inc(dst_x_made, 1)
                else:
                    dve.tensor_scalar(dst_hotT[c][:, :], dst_b[c][:, :], iota_p[:, 0:1], None,
                                      ALU.is_equal).then_inc(dst_hotT_made, 1)

            def rows(it, u, s):
                c = NS * u + s
                t = unit_chunk(it, u, s) * CT
                dve.tensor_tensor(lo_hot[c][:, :, :], iota_row[:, :].unsqueeze(1).broadcast_to((P, CT, P)),
                                  lo_f[:, bass.ds(t, CT)].unsqueeze(2).broadcast_to((P, CT, P)), ALU.is_equal)
                dve.tensor_tensor(hi_hot[c][:, :, :], iota_row[:, 0:NB].unsqueeze(1).broadcast_to((P, CT, NB)),
                                  hi_f[:, bass.ds(t, CT)].unsqueeze(2).broadcast_to((P, CT, NB)),
                                  ALU.is_equal).then_inc(hots_made, 1)

            def turn(it, last):
                for u in range(HALF):
                    half = HALF * it + u

                    def pick(m):
                        dve.wait_ge(looked, CT * half + m + 1)
                        for s in range(NS):
                            c = NS * u + s
                            dve.tensor_tensor_reduce(
                                out=picked[m % 2][s][:, :], in0=hi_hot[c][:, m, :],
                                in1=ps_look[m % 2][:, P * s:P * s + NB], scale=1.0, scalar=0.0, op0=ALU.mult,
                                op1=ALU.add, accum_out=place[c][:, m:m + 1]).then_inc(placed, 1)

                    nit, nu = (it, u + 1) if u + 1 < HALF else (it + 1, 0)
                    if not (last and nu == 0):
                        columns(nit, nu, 0)
                        pick(0)
                        columns(nit, nu, 1)
                        pick(1)
                        rows(nit, nu, 0)
                        pick(2)
                        rows(nit, nu, 1)
                    else:
                        for m in range(CT - 1):
                            pick(m)
                    for s in range(NS):
                        c = NS * u + s
                        dve.wait_ge(kv_copied, NU * it + c + 1)
                        dve.tensor_tensor(qk[s][:, :, :], ps_feat[s][:, :, KV:KV + DH], recs[c][:, :, 0:DH],
                                          ALU.mult).then_inc(dotted, 1)
                    pick(3)
                    for s in range(NS):
                        c = NS * u + s
                        dve.wait_ge(dotted, NU * it + c + 1)
                        dve.tensor_reduce(recs[c][:, :, KV:REC], qk[s][:, :, :].rearrange("p j (h d) -> p j h d", h=H),
                                          AX.X, ALU.add).then_inc(recs_made, 1)
                    for s in range(NS):
                        c = NS * u + s
                        dve.wait_ge(units_free, NU * it + c + 1)
                        dve.wait_ge(placed, 2 * NS + NS * CT * (half + 1))
                        dve.tensor_copy(place_i[c][:, :], place[c][:, :]).then_inc(places_made, 1)

            for s in range(NS):
                columns(0, 0, s)
                rows(0, 0, s)
            turns(dve, turn)

        def tensor_loop(pe, general):
            def match(it, u, m):
                half = HALF * it + u
                for s in range(NS):
                    pe.wait_ge(lo_hotT_made, NS * half + s + 1)
                if m or not isinstance(half, int) or half:
                    pe.wait_ge(masked, CT * half + m)
                nc.tensor.matmul(ps_eq[m % 2][:, 0:NS * P], ident_b[:, :], not_later[:, :, :], start=True, stop=False)
                for s in range(NS):
                    eT = lo_hotT[NS * u + s][:, P * m:P * (m + 1)]
                    last = nc.tensor.matmul(ps_eq[m % 2][:, P * s:P * (s + 1)], eT, eT, start=False, stop=(s == NS - 1))
                last.then_inc(matched, 1)

            def turn(it, last_turn):
                for u in range(HALF):
                    half = HALF * it + u

                    def attributes(s):
                        c = NS * u + s
                        pe.wait_ge(loaded[c], LOADS[general] * it + LOADS[general])
                        pe.wait_ge(recs_made, NS * half + s + 1)
                        nc.tensor.matmul(ps_feat[s][:, :, :], at[c][:, :], w_attr[:, :, :], start=True, stop=False)

                    def at_dst(s):
                        c = NS * u + s
                        if general:
                            pe.wait_ge(kv_got[c], 16 * CT * it + 16 * CT)
                        else:
                            pe.wait_ge(dst_hotT_made, NU * it + c + 1)
                        for j in range(CT):
                            hotT = ident[:, :] if general else dst_hotT[c][:, P * j:P * (j + 1)]
                            kv = kvg[c][:, j, :] if general else kvw[c][:, :]
                            last = nc.tensor.matmul(ps_feat[s][:, j, 0:KV], hotT, kv, start=False, stop=(j == CT - 1))
                        last.then_inc(feats, 1)

                    def look(m):
                        n = CT * half + m
                        pe.wait_ge(masked, 1 + n + 1)
                        pe.wait_ge(hots_made, NS * half + NS)
                        pe.wait_ge(placed, NS * n + NS)
                        for s in range(NS):
                            c = NS * u + s
                            pe.wait_ge(next_ready[s], n + 1)
                            g = ps_look[m % 2][:, P * s:P * s + NB]
                            nc.tensor.matmul(g, lo_hotT[c][:, P * m:P * (m + 1)], free_rec[s][:, :], start=True, stop=False)
                            last = nc.tensor.matmul(g, same[m % 2][:, s, :], hi_hot[c][:, m, :], start=False, stop=True)
                            if s == NS - 1:
                                last.then_inc(looked, 1)
                            nc.tensor.matmul(ps_cnt[s][:, 0:NB], lo_hot[c][:, m, :], hi_hot[c][:, m, :], start=False,
                                             stop=False, skip_group_check=True).then_inc(counted[s], 1)

                    nit, nu = (it, u + 1) if u + 1 < HALF else (it + 1, 0)
                    for m in range(CT):
                        if m + 1 < CT:
                            match(it, u, m + 1)
                        elif not (last_turn and nu == 0):
                            match(nit, nu, 0)
                        look(m)
                        if m < NS:
                            attributes(m)
                            at_dst(m)

            match(0, 0, 0)
            turns(pe, turn)

        def scalar_loop(act, general):
            def earlier(half, m):
                act.wait_ge(matched, CT * half + m + 1)
                act.activation(same[m % 2][:, :, :], ps_eq[m % 2][:, 0:NS * P].rearrange("p (s e) -> p s e", s=NS),
                               ACT.Relu).then_inc(masked, 1)

            def turn(it, last):
                for u in range(HALF):
                    half = HALF * it + u
                    for m in range(CT):
                        if m + 1 < CT:
                            earlier(half, m + 1)
                        elif not (last and u == HALF - 1):
                            earlier(half + 1, 0)
                        for s in range(NS):
                            act.wait_ge(counted[s], 1 + CT * half + m + 1)
                            act.activation(free_rec[s][:, :], ps_cnt[s][:, 0:NB], ACT.Copy).then_inc(next_ready[s], 1)
                        if 1 <= m <= NS:
                            s = m - 1
                            c = NS * u + s
                            act.wait_ge(feats, NU + NU * it + c + 1)
                            act.wait_ge(units_free, NU * it + c + 1)
                            act.activation(recs[c][:, :, 0:KV], ps_feat[s][:, :, 0:KV], ACT.Copy).then_inc(kv_copied, 1)

            earlier(0, 0)
            turns(act, turn)

        def both_ways(eng, loop):
            general = eng.value_load(flag[0:1, 0:1], min_val=0, max_val=1)
            with eng.If(general < 1):
                loop(eng, False)
            with eng.Else():
                loop(eng, True)

        block = ctx.enter_context(nc.Block())

        @block.sync
        def _(sp):
            sp.dma_start(dst_i[:, :], dst_tiles).then_inc(dst_in, 16)
            sp.wait_ge(ones_set, NU)
            both_ways(sp, load_loop)

        @block.gpsimd
        def _(pool):
            both_ways(pool, send_loop)

        @block.vector
        def _(dve):
            for s in range(NS):
                dve.tensor_single_scalar(not_later[:, s, :], later[:, :], -1.0, ALU.add).then_inc(consts, 1)
            dve.tensor_copy(ident_b[:, :], ident[:, :]).then_inc(consts, 1)
            for c in range(NU):
                dve.memset(at[c][:, :], 1.0).then_inc(ones_set, 1)
            dve.sem_inc(placed, 2 * NS)
            dve.sem_inc(recs_made, NS)
            dve.wait_ge(dst_in, 16)
            both_ways(dve, vector_loop)

        @block.tensor
        def _(pe):
            for s in range(NS):
                pe.sem_inc(counted[s], 1)
            pe.sem_inc(feats, NU)
            pe.wait_ge(consts, NS + 1)
            for s in range(NS):
                nc.tensor.matmul(ps_cnt[s][:, 0:NB], ident[:, :], base[:, s, :], start=True, stop=False,
                                 skip_group_check=True)
            both_ways(pe, tensor_loop)

        @block.scalar
        def _(act):
            act.sem_inc(masked, 1)
            for s in range(NS):
                act.activation(free_rec[s][:, :], base[:, s, :], ACT.Copy).then_inc(next_ready[s], 1)
            both_ways(act, scalar_loop)


def spread(table, chunk):
    return table[bass.ds(chunk, 1), :].partition_broadcast(P).rearrange("p a e -> p (a e)")


def attend_stage(nc, T, x, rec_dram, out):
    iota_f, ident, q_tab, base, deg = (T[k] for k in ("iota_f", "ident", "q_tab", "base", "deg"))
    with ExitStack() as ctx:
        def sb(name, shape, dt=F32):
            return ctx.enter_context(nc.sbuf_tensor(name, shape, dt))

        def sem(name):
            return ctx.enter_context(nc.semaphore(name))

        more_dram = nc.dram_tensor("more_dram", (NB,), I32, kind="Internal").ap()
        start_i = sb("start_i", [P, NB + 2], I32)
        most = sb("most", [NB, 1])
        more_i = sb("more_i", [NB, 1], I32)
        more = sb("more", [1, NB], I32)
        x_sb = sb("x_sb", [P, NB, DIM])
        y = sb("y", [P, NB, DIM])
        idx = [sb(f"idx{i}", [P, 1], I32) for i in range(2)]
        idx_x = sb("idx_x", [P, 1], I32)
        next_x = sb("next_x", [P, 1])
        left = sb("left", [P, 1])
        rec = [sb(f"rec{i}", [P, S0 * REC]) for i in range(2)]
        rec_x = sb("rec_x", [P, SX * REC])
        qk = sb("qk_s", [P, S0, DH])
        lg = sb("lg", [P, H, S0])
        past = sb("past", [P, S0])
        neg = sb("neg", [P, H])
        neg_x = sb("neg_x", [P, H])
        fall = sb("fall", [P, H])
        fall_e = sb("fall_e", [P, H])
        prob = sb("prob", [P, H, S0])
        den = sb("den", [P, H])
        den_x = sb("den_x", [P, H])
        msg = sb("msg", [P, S0, DIM])
        acc = sb("acc", [P, DIM])
        acc_x = sb("acc_x", [P, DIM])
        mean = sb("mean", [P, NB])
        rstd = sb("rstd", [P, NB])
        eps = sb("eps", [P, 1])
        ps_deg = ctx.enter_context(nc.psum_tensor("ps_deg", [NB, 512], F32))

        x_in, deg_up, more_made, more_out, more_in = (sem(n) for n in ("xs_in", "deg_up", "more_made", "more_out", "more_in"))
        idx_made = sem("idx_made")
        used = sem("used")
        rec_in = [sem(f"rec_in{i}") for i in range(2)]
        maxed, expd = sem("maxed"), sem("expd")
        steps = sem("block_steps")
        xi_made, xr_in, x_maxed, x_expd, x_steps = (sem(n) for n in ("xi_made", "xr_in", "x_maxed", "x_expd", "x_steps"))
        gathers = sem("gathers")
        ends, eps_set, rooted, normed, y_out = sem("ends"), sem("eps_set"), sem("rooted"), sem("normed"), sem("y_out")
        MAIN, MORE = 13, 16

        block = ctx.enter_context(nc.Block())

        @block.sync
        def _(sp):
            sp.dma_start(x_sb[:, :, :], x.rearrange("(b p) f -> p b f", p=P)).then_inc(x_in, 16)
            sp.wait_ge(more_made, 1)
            sp.dma_start(more_dram.rearrange("(b a) -> b a", a=1), more_i[:, :]).then_inc(more_out, 16)
            sp.wait_ge(more_out, 16)
            sp.dma_start(more[:, :], row_of(more_dram)).then_inc(more_in, 16)
            full = N // P
            sp.wait_ge(normed, 1)
            sp.dma_start(out[0:full * P, :].rearrange("(b p) f -> p b f", p=P), y[:, 0:full, :]).then_inc(y_out, 16)
            sp.dma_start(out[full * P:N, :], y[0:N - full * P, full, :]).then_inc(y_out, 16)
            sp.wait_ge(y_out, 32)

        @block.tensor
        def _(pe):
            nc.tensor.transpose(ps_deg[:, 0:P], deg[:, :], ident[:, :]).then_inc(deg_up, 1)

        @block.gpsimd
        def _(pool):
            for i in range(2):
                pool.wait_ge(idx_made, i + 1)
                pool.indirect_dma_start(rec[i][:, :], None, rec_dram[:, :],
                                        bass.IndirectOffsetOnAxis(idx[i][:, 0:1], 0)).then_inc(rec_in[i], 16)
            pool.wait_ge(more_in, 16)
            passes = pool.alloc_register("pool_passes")
            pool.reg_mov(passes, 0)
            with pool.Fori(0, NB // 2) as it:
                for i in range(2):
                    b = 2 * it + i
                    m = pool.value_load(more[0:1, bass.ds(b, 1)], min_val=0, max_val=EP)
                    with pool.If(m > 0):
                        with pool.Fori(0, m):
                            pool.wait_ge(xi_made, pool.snap(passes) + 1)
                            pool.sem_inc(gathers, 1)
                            pool.indirect_dma_start(rec_x[:, :], None, rec_dram[:, :],
                                                    bass.IndirectOffsetOnAxis(idx_x[:, 0:1], 0)).then_inc(xr_in, 16)
                            pool.reg_add(passes, passes, 1)
                    pool.wait_ge(idx_made, b + 3)
                    pool.wait_ge(used, b + 1)
                    pool.sem_inc(gathers, 1)
                    pool.indirect_dma_start(rec[i][:, :], None, rec_dram[:, :],
                                            bass.IndirectOffsetOnAxis(idx[i][:, 0:1], 0)).then_inc(rec_in[i], 16)
            for i in range(2):
                pool.wait_ge(rec_in[i], 16 * (NB // 2 + 1))

        @block.vector
        def _(dve):
            n = 0

            def end(ins):
                nonlocal n
                n += 1
                ins.then_inc(ends, 1)
                dve.wait_ge(ends, n)

            end(dve.memset(start_i[:, NB:NB + 2], 0))
            dve.memset(eps[:, :], 1e-5).then_inc(eps_set, 1)
            end(dve.tensor_copy(start_i[:, 0:NB], base[:, 0, :]))
            for i in range(2):
                dve.tensor_copy(idx[i][:, :], start_i[:, i:i + 1]).then_inc(idx_made, 1)
            dve.wait_ge(deg_up, 1)
            end(dve.reduce_max(most[:, :], ps_deg[:, 0:P], AX.X))
            end(dve.tensor_scalar(most[:, :], most[:, :], float(SX - 1 - S0), 0.0, ALU.add, ALU.max))
            end(dve.tensor_copy(more_i[:, :], most[:, :]))
            dve.tensor_single_scalar(more_i[:, :], more_i[:, :], int(math.log2(SX)), ALU.arith_shift_right).then_inc(more_made, 1)
            dve.wait_ge(x_in, 16)
            dve.wait_ge(more_in, 16)
            passes = dve.alloc_register("dve_passes")
            dve.reg_mov(passes, 0)

            def logits(r, slots, q, chain):
                v = r[:, :].rearrange("p (s f) -> p s f", f=REC)
                by_slot = lg[:, :, 0:slots].rearrange("p h s -> p s h")
                chain(dve.tensor_tensor(qk[:, 0:slots, :], v[:, :, 0:DH], q.broadcast_to((P, slots, DH)), ALU.mult))
                chain(dve.tensor_reduce(by_slot, qk[:, 0:slots, :].rearrange("p s (h d) -> p s h d", h=H), AX.X, ALU.add))
                chain(dve.tensor_tensor(by_slot, by_slot, v[:, :, KV:REC], ALU.add))
                chain(dve.tensor_tensor(lg[:, :, 0:slots], lg[:, :, 0:slots],
                                        past[:, 0:slots].unsqueeze(1).broadcast_to((P, H, slots)), ALU.add))

            def messages(r, slots):
                v = r[:, :].rearrange("p (s f) -> p s f", f=REC)
                return dve.tensor_tensor(
                    msg[:, 0:slots, :].rearrange("p s (h d) -> p s h d", h=H),
                    v[:, :, DH:KV].rearrange("p s (h d) -> p s h d", h=H),
                    prob[:, :, 0:slots].rearrange("p h s -> p s h").unsqueeze(3).broadcast_to((P, slots, H, VD)), ALU.mult)

            def summed(slots, total):
                return dve.tensor_reduce(total[:, :], msg[:, 0:slots, :].rearrange("p s f -> p f s"), AX.X, ALU.add)

            def by_head(t):
                return t.rearrange("p (h d) -> p h d", h=H)

            with dve.Fori(0, NB // 2) as it:
                for i in range(2):
                    b = 2 * it + i
                    k = 0

                    def chain(ins):
                        nonlocal k
                        k += 1
                        ins.then_inc(steps, 1)
                        dve.wait_ge(steps, MAIN * b + k)

                    dve.wait_ge(rec_in[i], 16 * it + 16)
                    dve.tensor_copy(idx[i][:, :], start_i[:, bass.ds(b + 2, 1)]).then_inc(idx_made, 1)
                    chain(dve.tensor_scalar(past[:, :], iota_f[:, 0:S0], deg[:, bass.ds(b, 1)], -BIG, ALU.is_ge, ALU.mult))
                    logits(rec[i], S0, q_tab[:, bass.ds(b, 1), :], chain)
                    chain(dve.tensor_reduce(neg[:, :], lg[:, :, :], AX.X, ALU.max, negate=True))
                    dve.tensor_single_scalar(neg[:, :], neg[:, :], BIG / 2, ALU.min).then_inc(maxed, 1)
                    chain(dve.tensor_single_scalar(left[:, :], deg[:, bass.ds(b, 1)], -float(S0), ALU.add))
                    chain(dve.tensor_scalar(next_x[:, :], base[:, 0, bass.ds(b, 1)], float(S0), float(EP), ALU.add, ALU.min))
                    dve.wait_ge(expd, b + 1)
                    messages(rec[i], S0).then_inc(used, 1)
                    dve.wait_ge(used, b + 1)
                    chain(summed(S0, acc))
                    m = dve.value_load(more[0:1, bass.ds(b, 1)], min_val=0, max_val=EP)
                    with dve.If(m > 0):
                        with dve.Fori(0, m):
                            done = dve.snap(passes)
                            kx = 0

                            def xchain(ins):
                                nonlocal kx
                                kx += 1
                                ins.then_inc(x_steps, 1)
                                dve.wait_ge(x_steps, MORE * done + kx)

                            dve.tensor_copy(idx_x[:, :], next_x[:, :]).then_inc(xi_made, 1)
                            xchain(dve.tensor_scalar(past[:, 0:SX], iota_f[:, 0:SX], left[:, 0:1], -BIG, ALU.is_ge, ALU.mult))
                            xchain(dve.tensor_scalar(next_x[:, :], next_x[:, :], float(SX), float(EP), ALU.add, ALU.min))
                            xchain(dve.tensor_single_scalar(left[:, :], left[:, :], -float(SX), ALU.add))
                            dve.wait_ge(xr_in, 16 * done + 16)
                            logits(rec_x, SX, q_tab[:, bass.ds(b, 1), :], xchain)
                            xchain(dve.tensor_reduce(neg_x[:, :], lg[:, :, 0:SX], AX.X, ALU.max, negate=True))
                            xchain(dve.tensor_tensor(neg_x[:, :], neg_x[:, :], neg[:, :], ALU.min))
                            dve.tensor_tensor(fall[:, :], neg_x[:, :], neg[:, :], ALU.subtract).then_inc(x_maxed, 1)
                            dve.wait_ge(x_maxed, done + 1)
                            xchain(dve.tensor_copy(neg[:, :], neg_x[:, :]))
                            dve.wait_ge(x_expd, done + 1)
                            xchain(dve.tensor_tensor(den[:, :], den[:, :], fall_e[:, :], ALU.mult))
                            xchain(dve.tensor_tensor(den[:, :], den[:, :], den_x[:, :], ALU.add))
                            xchain(dve.tensor_tensor(by_head(acc[:, :]), by_head(acc[:, :]),
                                                     fall_e[:, :].unsqueeze(2).broadcast_to((P, H, VD)), ALU.mult))
                            xchain(messages(rec_x, SX))
                            xchain(summed(SX, acc_x))
                            xchain(dve.tensor_tensor(acc[:, :], acc[:, :], acc_x[:, :], ALU.add))
                            assert kx == MORE, kx
                            dve.reg_add(passes, passes, 1)
                    chain(dve.tensor_single_scalar(den[:, :], den[:, :], 1e-16, ALU.add))
                    chain(dve.reciprocal(den[:, :], den[:, :]))
                    chain(dve.tensor_tensor(by_head(acc[:, :]), by_head(acc[:, :]),
                                            den[:, :].unsqueeze(2).broadcast_to((P, H, VD)), ALU.mult))
                    chain(dve.tensor_tensor(y[:, bass.ds(b, 1), :].rearrange("p a f -> p (a f)"), acc[:, :],
                                            x_sb[:, bass.ds(b, 1), :].rearrange("p a f -> p (a f)"), ALU.add))
                    assert k == MAIN, k
            end(dve.tensor_reduce(mean[:, :], y[:, :, :], AX.X, ALU.add))
            end(dve.tensor_single_scalar(mean[:, :], mean[:, :], 1.0 / DIM, ALU.mult))
            end(dve.tensor_tensor(y[:, :, :], y[:, :, :], mean[:, :].unsqueeze(2).broadcast_to((P, NB, DIM)), ALU.subtract))
            end(dve.tensor_tensor(x_sb[:, :, :], y[:, :, :], y[:, :, :], ALU.mult))
            end(dve.tensor_reduce(mean[:, :], x_sb[:, :, :], AX.X, ALU.add))
            dve.wait_ge(rooted, 1)
            end(dve.reciprocal(rstd[:, :], rstd[:, :]))
            dve.tensor_tensor(y[:, :, :], y[:, :, :], rstd[:, :].unsqueeze(2).broadcast_to((P, NB, DIM)),
                              ALU.mult).then_inc(normed, 1)
            assert n == 5 + 5 + 1, n

        @block.scalar
        def _(act):
            def exps(slots, negated, total, done):
                for h in range(H):
                    last = act.activation(prob[:, h, 0:slots], lg[:, h, 0:slots], ACT.Exp, bias=negated[:, h:h + 1],
                                          accum_out=total[:, h:h + 1])
                last.then_inc(done, 1)

            act.wait_ge(more_in, 16)
            passes = act.alloc_register("act_passes")
            act.reg_mov(passes, 0)
            with act.Fori(0, NB) as b:
                act.wait_ge(maxed, b + 1)
                exps(S0, neg, den, expd)
                m = act.value_load(more[0:1, bass.ds(b, 1)], min_val=0, max_val=EP)
                with act.If(m > 0):
                    with act.Fori(0, m):
                        act.wait_ge(x_maxed, act.snap(passes) + 1)
                        act.activation(fall_e[:, :], fall[:, :], ACT.Exp)
                        exps(SX, neg_x, den_x, x_expd)
                        act.reg_add(passes, passes, 1)
            act.wait_ge(eps_set, 1)
            act.wait_ge(ends, 10)
            act.activation(rstd[:, :], mean[:, :], ACT.Sqrt, bias=eps[:, 0:1], scale=1.0 / DIM).then_inc(rooted, 1)


def kernel(x, src, dst, edge_attr_18, L0_gnn_qkv_w, L0_gnn_qkv_b, L0_gnn_k_rpe_w, L0_gnn_k_rpe_b,
           L0_gnn_q_rpe_w, L0_gnn_q_rpe_b, L0_gnn_v_rpe_w, L0_gnn_v_rpe_b):
    import concourse.bacc as bacc
    from concourse.bass_utils import run_bass_kernel_spmd

    x, src, dst, attr = (np.asarray(a) for a in (x, src, dst, edge_attr_18))
    pad = (N + np.arange(EP - E) % (NN - N)).astype(np.int32)
    src = np.concatenate([src, pad])
    dst = np.concatenate([dst, pad])
    attr = np.concatenate([attr, np.zeros((EP - E, ATTR), attr.dtype)])
    x = np.concatenate([x, np.zeros((NN - N, DIM), x.dtype)])
    arrays = {
        "x": x,
        "xT": np.ascontiguousarray(x.T),
        "src_lin": src,
        "src_tiles": np.ascontiguousarray(src.reshape(NT, P).T),
        "dst_lin": dst,
        "dst_tiles": np.ascontiguousarray(dst.reshape(NT, P).T),
        "attr": np.ascontiguousarray(attr.reshape(NCH, CT, P, ATTR).transpose(0, 1, 3, 2)).reshape(NCH, CT * ATTR, P),
        "qkv_w": L0_gnn_qkv_w, "qkv_b": L0_gnn_qkv_b, "k_rpe_w": L0_gnn_k_rpe_w, "k_rpe_b": L0_gnn_k_rpe_b,
        "q_rpe_w": L0_gnn_q_rpe_w, "q_rpe_b": L0_gnn_q_rpe_b, "v_rpe_w": L0_gnn_v_rpe_w, "v_rpe_b": L0_gnn_v_rpe_b,
    }
    nc = bacc.Bacc("TRN2", target_bir_lowering=False, num_devices=1)
    feed, args = {}, []
    for name, a in arrays.items():
        a = np.ascontiguousarray(a)
        feed[f"in_{name}"] = a
        args.append(nc.dram_tensor(f"in_{name}", a.shape, mybir.dt.from_np(a.dtype), kind="ExternalInput").ap())
    args.append(nc.dram_tensor("out_y", (N, DIM), F32, kind="ExternalOutput").ap())
    gnn_kernel(nc, *args)
    r = run_bass_kernel_spmd(nc, [feed], core_ids=[0])
    return r.results[0]["out_y"]
```

```python
import math
from contextlib import ExitStack

import numpy as np
import concourse.bass as bass
from concourse import mybir

F32 = mybir.dt.float32
BF16 = mybir.dt.bfloat16
I32 = mybir.dt.int32
ALU = mybir.AluOpType
ACT = mybir.ActivationFunctionType
AX = mybir.AxisListType

P = 128
N, E = 12500, 412500
DIM, H, D = 64, 4, 8
DH, VD = H * D, DIM // H
ATTR = 18
NB = math.ceil(N / P)
NN = NB * P
CT = 4
CE = CT * P
NS = 2
HALF = 2
NCH = math.ceil(E / (CE * NS * HALF)) * NS * HALF
EP = NCH * CE
NT = NCH * CT
SC = NCH // NS
TURNS = SC // HALF
KV = DH + DIM
REC = KV + H
WP = 101
WG = NCH // WP
K_ROWS = CT * ATTR + 1
BIG = 1.0e30
S0 = 56
SP = 16
SUM = 8
RB = 4
GN = 14
SX = 16
RROWS = EP + S0 + SX
XG = 7
assert WP * WG == NCH and NCH % (NS * HALF) == 0 and NB % (2 * XG) == 0 and NT % (NS * 16) == 0 and NT // 32 % 2 == 1


def row_of(v):
    return v.rearrange("(a n) -> a n", a=1)


def gnn_kernel(nc, x, xT, src_lin, src_tiles, dst_lin, dst_tiles, attr, qkv_w, qkv_b, k_rpe_w, k_rpe_b,
               q_rpe_w, q_rpe_b, v_rpe_w, v_rpe_b, out):
    lo_dram = nc.dram_tensor("lo_dram", (NCH, CE), BF16, kind="Internal").ap()
    dl_dram = nc.dram_tensor("dl_dram", (NCH, CE), BF16, kind="Internal").ap()
    win_dram = nc.dram_tensor("win_dram", (NCH,), I32, kind="Internal").ap()
    over_dram = nc.dram_tensor("over_dram", (NCH,), F32, kind="Internal").ap()
    kv_dram = nc.dram_tensor("kv_dram", (NN, KV), F32, kind="Internal").ap()
    rec_dram = nc.dram_tensor("rec_dram", (RROWS, REC), F32, kind="Internal").ap()

    with ExitStack() as keep:
        def kept(name, shape, dt=F32):
            return keep.enter_context(nc.sbuf_tensor(name, shape, dt))

        T = dict(
            iota_row=kept("iota_row", [P, P], BF16),
            iota_f=kept("iota_f", [P, P]),
            iota_p=kept("iota_p", [P, 1]),
            ident=kept("ident", [P, P]),
            later=kept("later", [P, P]),
            q_tab=kept("q_tab", [P, NB, DH]),
            base=kept("base", [P, NS, NB]),
            deg=kept("deg", [P, NB]),
            w_attr=kept("w_attr", [P, CT, KV + DH]),
            win_row=kept("win_row", [1, NCH], I32),
            flag=kept("flag", [1, 1], I32),
        )
        digits = keep.enter_context(ExitStack())
        T["lo_f"] = digits.enter_context(nc.sbuf_tensor("lo_f", [P, NT], F32))
        T["hi_f"] = digits.enter_context(nc.sbuf_tensor("hi_f", [P, NT], F32))
        tables_stage(nc, T, xT, src_lin, src_tiles, dst_lin, qkv_w, qkv_b, k_rpe_w, k_rpe_b,
                     q_rpe_w, q_rpe_b, v_rpe_w, v_rpe_b, lo_dram, dl_dram, win_dram, over_dram, kv_dram,
                     rec_dram)
        sort_stage(nc, T, attr, dst_tiles, lo_dram, dl_dram, kv_dram, rec_dram)
        digits.close()
        attend_stage(nc, T, x, rec_dram, out)


def tables_stage(nc, T, xT, src_lin, src_tiles, dst_lin, qkv_w, qkv_b, k_rpe_w, k_rpe_b,
                 q_rpe_w, q_rpe_b, v_rpe_w, v_rpe_b, lo_dram, dl_dram, win_dram, over_dram, kv_dram,
                 rec_dram):
    iota_row, iota_f, iota_p, ident, later = (T[k] for k in ("iota_row", "iota_f", "iota_p", "ident", "later"))
    lo_f, hi_f, q_tab, base, deg, w_attr = (T[k] for k in ("lo_f", "hi_f", "q_tab", "base", "deg", "w_attr"))
    win_row, flag = T["win_row"], T["flag"]
    PER_TURN = 32
    GROUPS = ((0, 6), (6, 10), (16, 6), (22, 10))
    NG = len(GROUPS)
    COUNT_TURNS = NT // PER_TURN
    with ExitStack() as ctx:
        def sb(name, shape, dt=F32):
            return ctx.enter_context(nc.sbuf_tensor(name, shape, dt))

        def sem(name):
            return ctx.enter_context(nc.semaphore(name))

        iota_i = sb("iota_i", [P, P], I32)
        iota_pi = sb("iota_pi", [P, 1], I32)
        src_i = sb("src_i", [P, NT], I32)
        dig_i = sb("dig_i", [P, NT], I32)
        srcl_i = sb("srcl_i", [P, NT], I32)
        lo_lin = sb("lo_lin", [P, NT], BF16)
        dst_l = sb("dst_l", [WP, WG, CE], I32)
        dst_loc = sb("dst_loc", [WP, WG, CE], BF16)
        win_f = sb("win_f", [WP, WG])
        win_i = sb("win_i", [WP, WG], I32)
        over = sb("over", [WP, WG])
        over_row = sb("over_row", [1, NCH])
        flag_f = sb("flag_f", [1, 1])
        ones = sb("ones", [P, NB])
        incl = sb("incl", [P, NB])
        signs = sb("signs", [P, NS, NB + 1])
        row_base = sb("row_base", [P, 1])
        h_lo = [sb(f"h_lo{i}", [P, n, P], BF16) for i, (_, n) in enumerate(GROUPS)]
        s_hi = [sb(f"s_hi{i}", [P, n, NB + 1], BF16) for i, (_, n) in enumerate(GROUPS)]
        above = [sb(f"above{a}", [P, GROUPS[1][1], NB + 1], BF16) for a in range(2)]
        cols_half = sb("cols_half", [P, NB + 1])
        zeros = sb("zeros", [P, NS * (NB + 1)], BF16)
        w_qkv = sb("w_qkv", [DIM + 1, 2 * DH + DIM])
        xt = [sb(f"xt{i}", [DIM + 1, XG * P]) for i in range(2)]
        kvt = sb("kvt", [P, NB, KV])
        tail = sb("tail", [S0 + SX, REC])
        ps_hist = ctx.enter_context(nc.psum_tensor("ps_hist", [P, NS, 256], F32))
        ps_half = ctx.enter_context(nc.psum_tensor("ps_half", [P, 512], F32))
        ps_row = ctx.enter_context(nc.psum_tensor("ps_row", [P, 512], F32))
        ps_x = [ctx.enter_context(nc.psum_tensor(f"ps_x{i}", [P, 8, P], F32)) for i in range(2)]

        src_in, srcl_in, dst_in = sem("src_in"), sem("srcl_in"), sem("dst_in")
        w_zero, w_in, x_ones = sem("w_zero"), sem("w_in"), sem("x_ones")
        iotas, consts, diag = sem("iotas"), sem("consts"), sem("diag")
        steps = sem("steps")
        lo_made, lo_out = sem("lo_made"), sem("lo_out")
        loc_made, loc_out = sem("loc_made"), sem("loc_out")
        win_made, win_out, win_in, flag_made = sem("win_made"), sem("win_out"), sem("win_in"), sem("flag_made")
        digits_made, half_made, half_copied = sem("digits_made"), sem("half_made"), sem("half_copied")
        subtracted = sem("subtracted")
        lo_rows, hi_signs, tallied = sem("lo_rows"), sem("hi_signs"), sem("tallied")
        sums_made, rows_summed = sem("sums_made"), sem("rows_summed")
        tail_zero, tail_out = sem("tail_zero"), sem("tail_out")
        x_in = [sem(f"x_in{i}") for i in range(2)]
        x_done, q_read = sem("x_done"), sem("q_read")
        kv_made = sem("kv_made")
        kv_out = sem("kv_out")
        n_w = 2 + 6 * CT

        block = ctx.enter_context(nc.Block())

        @block.sync
        def _(sp):
            sp.dma_start(src_i[:, :], src_tiles).then_inc(src_in, 16)
            sp.dma_start(srcl_i[:, :], src_lin.rearrange("(p t) -> p t", p=P)).then_inc(srcl_in, 16)
            sp.dma_start(dst_l[:, :, :], dst_lin.rearrange("(p g e) -> p g e", p=WP, g=WG)).then_inc(dst_in, 16)
            sp.dma_start(w_qkv[0:DIM, :], qkv_w).then_inc(w_in, 16)
            sp.dma_start(w_qkv[DIM:DIM + 1, :], row_of(qkv_b)).then_inc(w_in, 16)
            sp.wait_ge(w_zero, 1)
            for j in range(CT):
                for c, w, b in ((0, k_rpe_w, k_rpe_b), (DH, v_rpe_w, v_rpe_b), (KV, q_rpe_w, q_rpe_b)):
                    n = w.shape[1]
                    sp.dma_start(w_attr[ATTR * j:ATTR * (j + 1), j, c:c + n], w).then_inc(w_in, 16)
                    sp.dma_start(w_attr[K_ROWS - 1:K_ROWS, j, c:c + n], row_of(b)).then_inc(w_in, 16)
            sp.wait_ge(x_ones, 2)
            with sp.Fori(0, NB // (2 * XG)) as it:
                for i in range(2):
                    sp.wait_ge(x_done, 2 * it + i + 1)
                    sp.dma_start(xt[i][0:DIM, :], xT[:, bass.ds((2 * it + i) * XG * P, XG * P)]).then_inc(x_in[i], 16)
            sp.wait_ge(lo_made, 1)
            sp.dma_start(lo_dram.rearrange("c e -> (c e)").rearrange("(p t) -> p t", p=P), lo_lin[:, :]).then_inc(lo_out, 16)
            sp.wait_ge(loc_made, WG)
            sp.dma_start(dl_dram.rearrange("(p g) e -> p g e", p=WP), dst_loc[:, :, :]).then_inc(loc_out, 16)
            sp.wait_ge(win_made, 2)
            sp.dma_start(win_dram.rearrange("(p g) -> p g", p=WP), win_i[:, :]).then_inc(win_out, 16)
            sp.dma_start(over_dram.rearrange("(p g) -> p g", p=WP), over[:, :]).then_inc(win_out, 16)
            sp.wait_ge(win_out, 32)
            sp.dma_start(win_row[:, :], row_of(win_dram)).then_inc(win_in, 16)
            sp.dma_start(over_row[:, :], row_of(over_dram)).then_inc(win_in, 16)
            sp.wait_ge(kv_made, NB // XG)
            sp.dma_start(kv_dram.rearrange("(b p) f -> p b f", p=P), kvt[:, :, :]).then_inc(kv_out, 16)
            sp.wait_ge(kv_out, 16)
            sp.wait_ge(tail_zero, 1)
            sp.dma_start(rec_dram[EP:RROWS, :], tail[:, :]).then_inc(tail_out, 16)
            sp.wait_ge(tail_out, 16)
            sp.wait_ge(lo_out, 16)
            sp.wait_ge(loc_out, 16)
            sp.wait_ge(win_in, 32)
            sp.wait_ge(w_in, 16 * n_w)

        @block.gpsimd
        def _(pool):
            pool.iota(iota_i[:, :], pattern=[[1, P]], base=0, channel_multiplier=0).then_inc(iotas, 1)
            pool.iota(iota_pi[:, :], pattern=[[0, 1]], base=0, channel_multiplier=1).then_inc(iotas, 1)
            pool.memset(ident[:, :], 0.0).then_inc(diag, 1)
            pool.memset(later[:, :], 1.0).then_inc(diag, 1)
            pool.wait_ge(diag, 2)
            pool.affine_select(out=ident[:, :], in_=ident[:, :], compare_op=ALU.not_equal, fill=1.0,
                               base=0, pattern=[[-1, P]], channel_multiplier=1).then_inc(diag, 1)
            pool.affine_select(out=later[:, :], in_=later[:, :], compare_op=ALU.is_gt, fill=0.0,
                               base=0, pattern=[[1, P]], channel_multiplier=-1).then_inc(diag, 1)
            pool.wait_ge(diag, 4)
            pool.wait_ge(digits_made, 1)
            pool.wait_ge(half_made, 1)
            with pool.Fori(0, COUNT_TURNS) as it:
                for i in (1, 3):
                    first, n = GROUPS[i]
                    pool.wait_ge(hi_signs, NG * it + i + 1)
                    pool.tensor_tensor(above[i // 2][:, :, :],
                                       hi_f[:, bass.ds(PER_TURN * it + first, n)].unsqueeze(2).broadcast_to((P, n, NB + 1)),
                                       cols_half[:, :].unsqueeze(1).broadcast_to((P, n, NB + 1)),
                                       ALU.subtract).then_inc(subtracted, 1)

        @block.vector
        def _(dve):
            dve.memset(w_attr[:, :, :], 0.0).then_inc(w_zero, 1)
            dve.memset(xt[0][DIM:DIM + 1, :], 1.0).then_inc(x_ones, 1)
            dve.memset(xt[1][DIM:DIM + 1, :], 1.0).then_inc(x_ones, 1)
            dve.memset(tail[:, :], 0.0).then_inc(tail_zero, 1)
            dve.memset(ones[:, :], 1.0).then_inc(consts, 1)
            dve.memset(zeros[:, :], 0.0).then_inc(consts, 1)
            dve.wait_ge(iotas, 2)
            dve.tensor_copy(iota_row[:, :], iota_i[:, :]).then_inc(consts, 1)
            dve.tensor_copy(iota_f[:, :], iota_i[:, :]).then_inc(consts, 1)
            dve.tensor_copy(iota_p[:, :], iota_pi[:, :]).then_inc(consts, 1)
            n = 0

            def step(ins):
                nonlocal n
                n += 1
                ins.then_inc(steps, 1)
                dve.wait_ge(steps, n)

            dve.wait_ge(src_in, 16)
            step(dve.tensor_single_scalar(dig_i[:, :], src_i[:, :], P - 1, ALU.bitwise_and))
            step(dve.tensor_copy(lo_f[:, :], dig_i[:, :]))
            step(dve.tensor_single_scalar(dig_i[:, :], src_i[:, :], 7, ALU.arith_shift_right))
            dve.tensor_copy(hi_f[:, :], dig_i[:, :]).then_inc(digits_made, 1)
            dve.wait_ge(digits_made, 1)
            dve.wait_ge(consts, 5)
            dve.tensor_single_scalar(cols_half[:, :], iota_f[:, 0:NB + 1], -0.5, ALU.add).then_inc(half_made, 1)
            dve.wait_ge(srcl_in, 16)
            step(dve.tensor_single_scalar(dig_i[:, :], srcl_i[:, :], P - 1, ALU.bitwise_and))
            dve.tensor_copy(lo_lin[:, :], dig_i[:, :]).then_inc(lo_made, 1)
            dve.wait_ge(dst_in, 16)
            step(dve.tensor_reduce(win_f[:, :], dst_l[:, :, :], AX.X, ALU.min))
            step(dve.tensor_single_scalar(win_f[:, :], win_f[:, :], float(NN - P), ALU.min))
            step(dve.tensor_reduce(over[:, :], dst_l[:, :, :], AX.X, ALU.max))
            dve.tensor_copy(win_i[:, :], win_f[:, :]).then_inc(win_made, 1)
            dve.tensor_sub(over[:, :], over[:, :], win_f[:, :]).then_inc(win_made, 1)
            for g in range(WG):
                dve.tensor_scalar(dst_loc[:, g, :], dst_l[:, g, :], win_f[:, g:g + 1], None,
                                  ALU.subtract).then_inc(loc_made, 1)
            with dve.Fori(0, COUNT_TURNS) as it:
                for i, (first, n_tiles) in enumerate(GROUPS):
                    dve.wait_ge(tallied, NG * it + i + 1)
                    dve.tensor_tensor(h_lo[i][:, :, :], iota_row[:, :].unsqueeze(1).broadcast_to((P, n_tiles, P)),
                                      lo_f[:, bass.ds(PER_TURN * it + first, n_tiles)].unsqueeze(2).broadcast_to((P, n_tiles, P)),
                                      ALU.is_equal).then_inc(lo_rows, 1)
            dve.wait_ge(win_in, 32)
            step(dve.reduce_max(flag_f[:, :], over_row[:, :], AX.X))
            step(dve.tensor_single_scalar(flag_f[:, :], flag_f[:, :], float(P), ALU.is_ge))
            dve.tensor_copy(flag[:, :], flag_f[:, :]).then_inc(flag_made, 1)
            dve.wait_ge(tallied, NG + NG * COUNT_TURNS)
            step(dve.tensor_copy(signs[:, :, :], ps_hist[:, :, 0:NB + 1]))
            step(dve.tensor_sub(base[:, :, :], signs[:, :, 0:NB], signs[:, :, 1:NB + 1]))
            step(dve.tensor_single_scalar(base[:, :, :], base[:, :, :], 0.5, ALU.mult))
            step(dve.tensor_add(deg[:, :], base[:, 0, :], base[:, 1, :]))
            step(dve.tensor_tensor_scan(incl[:, :], ones[:, :], deg[:, :], 0.0, ALU.mult, ALU.add))
            sums = dve.tensor_sub(incl[:, 0:NB - 1], incl[:, 0:NB - 1], deg[:, 0:NB - 1])
            sums.then_inc(sums_made, 1)
            dve.wait_ge(sums_made, 1)
            dve.wait_ge(rows_summed, 1)
            step(dve.tensor_copy(row_base[:, :], ps_row[:, 0:1]))
            step(dve.tensor_sub(incl[:, NB - 1:NB], incl[:, NB - 1:NB], deg[:, NB - 1:NB]))
            step(dve.tensor_scalar(incl[:, :], incl[:, :], row_base[:, 0:1], None, ALU.add))
            step(dve.tensor_add(base[:, 1, :], base[:, 0, :], incl[:, :]))
            step(dve.tensor_copy(base[:, 0, :], incl[:, :]))
            dve.wait_ge(loc_made, WG)
            dve.wait_ge(flag_made, 1)
            dve.wait_ge(lo_made, 1)

        @block.tensor
        def _(pe):
            pe.sem_inc(x_done, 2)
            pe.sem_inc(tallied, NG)
            pe.wait_ge(w_in, 16 * n_w)
            with pe.Fori(0, NB // (2 * XG)) as it:
                for i in range(2):
                    pe.wait_ge(x_in[i], 16 * it + 16)
                    pe.wait_ge(q_read, 2 * it + i + 1)
                    for b in range(XG):
                        last = nc.tensor.matmul(ps_x[i][:, b, :], xt[i][:, b * P:(b + 1) * P], w_qkv[:, :],
                                                start=True, stop=True)
                    last.then_inc(x_done, 1)
            pe.wait_ge(consts, 5)
            nc.tensor.matmul(ps_hist[:, :, 0:NB + 1], zeros[:, 0:P], zeros[:, :].rearrange("p (s b) -> p s b", s=NS),
                             start=True, stop=False, skip_group_check=True)
            def tally(it, streams):
                for i, (_, n_tiles) in enumerate(GROUPS):
                    pe.wait_ge(lo_rows, NG * it + i + 1)
                    pe.wait_ge(hi_signs, NG + NG * it + i + 1)
                    for k in range(n_tiles):
                        last = nc.tensor.matmul(ps_hist[:, streams[i], 0:NB + 1], h_lo[i][:, k, :], s_hi[i][:, k, :],
                                                start=False, stop=False, skip_group_check=True)
                    last.then_inc(tallied, 1)

            with pe.Fori(0, COUNT_TURNS // 2) as it:
                tally(it, (0, 0, 0, 0))
            tally(COUNT_TURNS // 2, (0, 0, 1, 1))
            with pe.Fori(COUNT_TURNS // 2 + 1, COUNT_TURNS) as it:
                tally(it, (1, 1, 1, 1))
            pe.wait_ge(sums_made, 1)
            pe.wait_ge(diag, 4)
            nc.tensor.matmul(ps_row[:, 0:1], later[:, :], incl[:, NB - 1:NB], start=True,
                             stop=True).then_inc(rows_summed, 1)

        @block.scalar
        def _(act):
            act.sem_inc(q_read, 2)
            act.sem_inc(hi_signs, NG)
            with act.Fori(0, NB // (2 * XG)) as it:
                for i in range(2):
                    act.wait_ge(x_done, 2 + 2 * it + i + 1)
                    act.activation(kvt[:, bass.ds((2 * it + i) * XG, XG), :], ps_x[i][:, 0:XG, DH:DH + KV], ACT.Copy).then_inc(kv_made, 1)
                    act.activation(q_tab[:, bass.ds((2 * it + i) * XG, XG), :], ps_x[i][:, 0:XG, 0:DH], ACT.Copy,
                                   scale=float(D) ** -0.5).then_inc(q_read, 1)
            act.wait_ge(half_made, 1)
            act.wait_ge(digits_made, 1)
            act.activation(ps_half[:, 0:NB + 1], cols_half[:, :], ACT.Copy).then_inc(half_copied, 1)
            act.wait_ge(half_copied, 1)
            with act.Fori(0, COUNT_TURNS) as it:
                for i, (first, n_tiles) in enumerate(GROUPS):
                    act.wait_ge(tallied, NG * it + i + 1)
                    if i % 2:
                        act.wait_ge(subtracted, 2 * it + i // 2 + 1)
                        last = act.activation(s_hi[i][:, :, :], above[i // 2][:, :, :], ACT.Sign)
                    else:
                        for k in range(n_tiles):
                            last = act.activation(s_hi[i][:, k, :], ps_half[:, 0:NB + 1], ACT.Sign, scale=-1.0,
                                                  bias=hi_f[:, bass.ds(PER_TURN * it + first + k, 1)])
                    last.then_inc(hi_signs, 1)


def sort_stage(nc, T, attr, dst_tiles, lo_dram, dl_dram, kv_dram, rec_dram):
    iota_row, iota_f, iota_p, ident, later = (T[k] for k in ("iota_row", "iota_f", "iota_p", "ident", "later"))
    lo_f, hi_f, base, w_attr, win_row, flag = (T[k] for k in ("lo_f", "hi_f", "base", "w_attr", "win_row", "flag"))
    FEATURES = (0, 2)
    UNITS = [(u, s) for u in range(HALF) for s in range(NS)]
    with ExitStack() as ctx:
        def sb(name, shape, dt=F32):
            return ctx.enter_context(nc.sbuf_tensor(name, shape, dt))

        def sem(name):
            return ctx.enter_context(nc.semaphore(name))

        NU = len(UNITS)
        dst_i = sb("dst_i", [P, NT], I32)
        lo_b = [sb(f"lo_b{c}", [P, CE], BF16) for c in range(NU)]
        dst_b = [sb(f"dst_b{c}", [P, CE], BF16) for c in range(NU)]
        at = [sb(f"at{c}", [P, P]) for c in range(NU)]
        kvw = [sb(f"kvw{c}", [P, KV]) for c in range(NU)]
        kvg = [sb(f"kvg{c}", [P, CT, KV]) for c in range(NU)]
        dst_x = [sb(f"dst_x{c}", [P, CT], I32) for c in range(NU)]
        lo_hotT = [sb(f"lo_hotT{c}", [P, CE]) for c in range(NU)]
        dst_hotT = [sb(f"dst_hotT{c}", [P, CE]) for c in range(NU)]
        lo_hot = [sb(f"lo_hot{c}", [P, CT, P], BF16) for c in range(NU)]
        hi_hot = [sb(f"hi_hot{c}", [P, CT, NB], BF16) for c in range(NU)]
        same = [sb(f"same{i}", [P, NS, P], BF16) for i in range(2)]
        free_rec = [sb(f"free_rec{s}", [P, NB]) for s in range(NS)]
        picked = [[sb(f"picked{i}{s}", [P, NB]) for s in range(NS)] for i in range(2)]
        place = [sb(f"place{c}", [P, CT]) for c in range(NU)]
        place_i = [sb(f"place_i{c}", [P, CT], I32) for c in range(NU)]
        recs = [sb(f"recs{c}", [P, CT, REC]) for c in range(NU)]
        qk = [sb(f"qk{s}", [P, CT, DH]) for s in range(NS)]
        not_later = sb("not_later", [P, NS, P], BF16)
        ident_b = sb("ident_b", [P, P], BF16)

        def pb(name, shape):
            return ctx.enter_context(nc.psum_tensor(name, shape, F32))

        ps_cnt = [pb(f"ps_cnt{s}", [P, 512]) for s in range(NS)]
        ps_feat = [pb(f"ps_feat{s}", [P, CT, KV + DH]) for s in range(2)]
        ps_eq = [pb(f"ps_eq{i}", [P, 512]) for i in range(2)]
        ps_look = [pb(f"ps_look{i}", [P, 512]) for i in range(2)]

        consts, ones_set, dst_in = sem("sort_consts"), sem("ones_set"), sem("sort_dst_in")
        loaded = [sem(f"loaded{c}") for c in range(NU)]
        lo_hotT_made, dst_hotT_made, hots_made = sem("lo_hotT_made"), sem("dst_hotT_made"), sem("hots_made")
        dst_x_made = sem("dst_x_made")
        kv_got = [sem(f"kv_got{c}") for c in range(NU)]
        feats = sem("feats")
        kv_copied, dotted = sem("kv_copied"), sem("dotted")
        recs_made = sem("recs_made")
        units_free = sem("units_free")
        matched, looked = sem("matched"), sem("looked")
        masked = sem("masked")
        placed = sem("placed")
        counted = [sem(f"counted{s}") for s in range(NS)]
        next_ready = [sem(f"next_ready{s}") for s in range(NS)]
        places_made = sem("places_made")
        scattered = [sem(f"scattered{c}") for c in range(NU)]
        chunks_sent = sem("chunks_sent")
        LOADS = {False: 16 * 4, True: 16 * 2}

        def unit_chunk(it, u, s):
            return s * SC + it * HALF + u

        def turns(eng, turn):
            with eng.Fori(0, TURNS - 1) as it:
                turn(it, False)
            turn(TURNS - 1, True)

        def load_loop(sp, general):
            if general:
                sp.dma_start(dst_i[:, :], dst_tiles).then_inc(dst_in, 16)
            with sp.Fori(0, TURNS) as it:
                for c, (u, s) in enumerate(UNITS):
                    chunk = unit_chunk(it, u, s)
                    sp.wait_ge(feats, NU * it + c + 1)
                    sp.dma_start(at[c][0:K_ROWS - 1, :],
                                 attr[bass.ds(chunk, 1), :, :].rearrange("a k e -> (a k) e")).then_inc(loaded[c], 16)
                    sp.dma_start(lo_b[c][:, :], spread(lo_dram, chunk)).then_inc(loaded[c], 16)
                    if not general:
                        sp.dma_start(dst_b[c][:, :], spread(dl_dram, chunk)).then_inc(loaded[c], 16)
                        w = sp.value_load(win_row[0:1, bass.ds(chunk, 1)], min_val=0, max_val=NN - P)
                        sp.dma_start(kvw[c][:, :], kv_dram[bass.ds(w, P), :]).then_inc(loaded[c], 16)

        def send_loop(pool, general):
            def turn(it, first):
                for u in range(HALF):
                    for c in range(NS * u, NS * u + NS):
                        if general:
                            pool.wait_ge(dst_x_made, NU * it + c + 1)
                            pool.sem_inc(chunks_sent, 1)
                            for j in range(CT):
                                pool.indirect_dma_start(kvg[c][:, j, :], None, kv_dram,
                                                        bass.IndirectOffsetOnAxis(dst_x[c][:, j:j + 1], 0)).then_inc(kv_got[c], 16)
                    for c in range(NS * u, NS * u + NS):
                        pool.wait_ge(recs_made, NS + NU * it + c + 1)
                        pool.wait_ge(kv_copied, NU * it + c + 1)
                        pool.wait_ge(places_made, NU * it + c + 1)
                        pool.sem_inc(chunks_sent, 1)
                        for j in range(CT):
                            pool.indirect_dma_start(rec_dram[:, :], bass.IndirectOffsetOnAxis(place_i[c][:, j:j + 1], 0),
                                                    recs[c][:, j, :], None).then_inc(scattered[c], 16)
                        if c:
                            pool.wait_ge(scattered[c - 1], 16 * CT * it + 16 * CT)
                            pool.sem_inc(units_free, 1)
                        elif not first:
                            pool.wait_ge(scattered[NU - 1], 16 * CT * it)
                            pool.sem_inc(units_free, 1)

            pool.sem_inc(units_free, NU)
            turn(0, True)
            with pool.Fori(1, TURNS) as it:
                turn(it, False)
            pool.wait_ge(scattered[NU - 1], 16 * CT * TURNS)

        def vector_loop(dve, general):
            def columns(it, u, s):
                c = NS * u + s
                half = HALF * it + u
                dve.wait_ge(loaded[c], LOADS[general] * it + LOADS[general])
                if not (isinstance(half, int) and half == 0):
                    dve.wait_ge(counted[s], 1 + CT * (half - 1))
                dve.tensor_scalar(lo_hotT[c][:, :], lo_b[c][:, :], iota_p[:, 0:1], None, ALU.is_equal).then_inc(lo_hotT_made, 1)
                dve.wait_ge(feats, NU * it + c + 1)
                if general:
                    dve.tensor_copy(dst_x[c][:, :], dst_i[:, bass.ds(unit_chunk(it, u, s) * CT, CT)]).then_inc(dst_x_made, 1)
                else:
                    dve.tensor_scalar(dst_hotT[c][:, :], dst_b[c][:, :], iota_p[:, 0:1], None,
                                      ALU.is_equal).then_inc(dst_hotT_made, 1)

            def rows(it, u, s):
                c = NS * u + s
                t = unit_chunk(it, u, s) * CT
                dve.tensor_tensor(lo_hot[c][:, :, :], iota_row[:, :].unsqueeze(1).broadcast_to((P, CT, P)),
                                  lo_f[:, bass.ds(t, CT)].unsqueeze(2).broadcast_to((P, CT, P)), ALU.is_equal)
                dve.tensor_tensor(hi_hot[c][:, :, :], iota_row[:, 0:NB].unsqueeze(1).broadcast_to((P, CT, NB)),
                                  hi_f[:, bass.ds(t, CT)].unsqueeze(2).broadcast_to((P, CT, NB)),
                                  ALU.is_equal).then_inc(hots_made, 1)

            def turn(it, last):
                for u in range(HALF):
                    half = HALF * it + u

                    def pick(m):
                        dve.wait_ge(looked, CT * half + m + 1)
                        for s in range(NS):
                            c = NS * u + s
                            dve.tensor_tensor_reduce(
                                out=picked[m % 2][s][:, :], in0=hi_hot[c][:, m, :],
                                in1=ps_look[m % 2][:, P * s:P * s + NB], scale=1.0, scalar=0.0, op0=ALU.mult,
                                op1=ALU.add, accum_out=place[c][:, m:m + 1]).then_inc(placed, 1)

                    nit, nu = (it, u + 1) if u + 1 < HALF else (it + 1, 0)
                    if not (last and nu == 0):
                        columns(nit, nu, 0)
                        pick(0)
                        columns(nit, nu, 1)
                        pick(1)
                        rows(nit, nu, 0)
                        pick(2)
                        rows(nit, nu, 1)
                    else:
                        for m in range(CT - 1):
                            pick(m)
                    pick(3)
                    for s in range(NS):
                        c = NS * u + s
                        dve.wait_ge(kv_copied, NU * it + c + 1)
                        dve.tensor_tensor(qk[s][:, :, :], ps_feat[s][:, :, KV:KV + DH], recs[c][:, :, 0:DH],
                                          ALU.mult).then_inc(dotted, 1)
                    for s in range(NS):
                        c = NS * u + s
                        dve.wait_ge(dotted, NU * it + c + 1)
                        dve.tensor_reduce(recs[c][:, :, KV:REC], qk[s][:, :, :].rearrange("p j (h d) -> p j h d", h=H),
                                          AX.X, ALU.add).then_inc(recs_made, 1)
                    for s in range(NS):
                        c = NS * u + s
                        dve.wait_ge(units_free, NU * it + c + 1)
                        dve.wait_ge(placed, 2 * NS + NS * CT * (half + 1))
                        dve.tensor_copy(place_i[c][:, :], place[c][:, :]).then_inc(places_made, 1)

            if general:
                dve.wait_ge(dst_in, 16)
            for s in range(NS):
                columns(0, 0, s)
                rows(0, 0, s)
            turns(dve, turn)

        def tensor_loop(pe, general):
            def match(it, u, m):
                half = HALF * it + u
                for s in range(NS):
                    pe.wait_ge(lo_hotT_made, NS * half + s + 1)
                if m or not isinstance(half, int) or half:
                    pe.wait_ge(masked, CT * half + m)
                nc.tensor.matmul(ps_eq[m % 2][:, 0:NS * P], ident_b[:, :], not_later[:, :, :], start=True, stop=False)
                for s in range(NS):
                    eT = lo_hotT[NS * u + s][:, P * m:P * (m + 1)]
                    last = nc.tensor.matmul(ps_eq[m % 2][:, P * s:P * (s + 1)], eT, eT, start=False, stop=(s == NS - 1))
                last.then_inc(matched, 1)

            def turn(it, last_turn):
                for u in range(HALF):
                    half = HALF * it + u

                    def attributes(s):
                        c = NS * u + s
                        pe.wait_ge(loaded[c], LOADS[general] * it + LOADS[general])
                        pe.wait_ge(recs_made, NS * half + s + 1)
                        nc.tensor.matmul(ps_feat[s][:, :, :], at[c][:, :], w_attr[:, :, :], start=True, stop=False)

                    def at_dst(s):
                        c = NS * u + s
                        if general:
                            pe.wait_ge(kv_got[c], 16 * CT * it + 16 * CT)
                        else:
                            pe.wait_ge(dst_hotT_made, NU * it + c + 1)
                        for j in range(CT):
                            hotT = ident[:, :] if general else dst_hotT[c][:, P * j:P * (j + 1)]
                            kv = kvg[c][:, j, :] if general else kvw[c][:, :]
                            last = nc.tensor.matmul(ps_feat[s][:, j, 0:KV], hotT, kv, start=False, stop=(j == CT - 1))
                        last.then_inc(feats, 1)

                    def look(m):
                        n = CT * half + m
                        pe.wait_ge(masked, 1 + n + 1)
                        pe.wait_ge(hots_made, NS * half + NS)
                        pe.wait_ge(placed, NS * n + NS)
                        for s in range(NS):
                            c = NS * u + s
                            pe.wait_ge(next_ready[s], n + 1)
                            g = ps_look[m % 2][:, P * s:P * s + NB]
                            nc.tensor.matmul(g, lo_hotT[c][:, P * m:P * (m + 1)], free_rec[s][:, :], start=True, stop=False)
                            last = nc.tensor.matmul(g, same[m % 2][:, s, :], hi_hot[c][:, m, :], start=False, stop=True)
                            if s == NS - 1:
                                last.then_inc(looked, 1)
                            nc.tensor.matmul(ps_cnt[s][:, 0:NB], lo_hot[c][:, m, :], hi_hot[c][:, m, :], start=False,
                                             stop=False, skip_group_check=True).then_inc(counted[s], 1)

                    nit, nu = (it, u + 1) if u + 1 < HALF else (it + 1, 0)
                    for m in range(CT):
                        if m + 1 < CT:
                            match(it, u, m + 1)
                        elif not (last_turn and nu == 0):
                            match(nit, nu, 0)
                        look(m)
                        if m in FEATURES:
                            attributes(FEATURES.index(m))
                            at_dst(FEATURES.index(m))

            match(0, 0, 0)
            turns(pe, turn)

        def scalar_loop(act, general):
            def earlier(half, m):
                act.wait_ge(matched, CT * half + m + 1)
                act.activation(same[m % 2][:, :, :], ps_eq[m % 2][:, 0:NS * P].rearrange("p (s e) -> p s e", s=NS),
                               ACT.Relu).then_inc(masked, 1)

            def turn(it, last):
                for u in range(HALF):
                    half = HALF * it + u
                    for m in range(CT):
                        if m + 1 < CT:
                            earlier(half, m + 1)
                        elif not (last and u == HALF - 1):
                            earlier(half + 1, 0)
                        if m - 1 in FEATURES:
                            s = FEATURES.index(m - 1)
                            c = NS * u + s
                            act.wait_ge(feats, NU + NU * it + c + 1)
                            act.wait_ge(units_free, NU * it + c + 1)
                            act.activation(recs[c][:, :, 0:KV], ps_feat[s][:, :, 0:KV], ACT.Copy).then_inc(kv_copied, 1)
                        for s in range(NS):
                            act.wait_ge(counted[s], 1 + CT * half + m + 1)
                            act.activation(free_rec[s][:, :], ps_cnt[s][:, 0:NB], ACT.Copy).then_inc(next_ready[s], 1)

            earlier(0, 0)
            turns(act, turn)

        def both_ways(eng, loop):
            general = eng.value_load(flag[0:1, 0:1], min_val=0, max_val=1)
            with eng.If(general < 1):
                loop(eng, False)
            with eng.Else():
                loop(eng, True)

        block = ctx.enter_context(nc.Block())

        @block.sync
        def _(sp):
            sp.wait_ge(ones_set, NU)
            both_ways(sp, load_loop)

        @block.gpsimd
        def _(pool):
            both_ways(pool, send_loop)

        @block.vector
        def _(dve):
            for s in range(NS):
                dve.tensor_single_scalar(not_later[:, s, :], later[:, :], -1.0, ALU.add).then_inc(consts, 1)
            dve.tensor_copy(ident_b[:, :], ident[:, :]).then_inc(consts, 1)
            for c in range(NU):
                dve.memset(at[c][:, :], 1.0).then_inc(ones_set, 1)
            dve.sem_inc(placed, 2 * NS)
            dve.sem_inc(recs_made, NS)
            both_ways(dve, vector_loop)

        @block.tensor
        def _(pe):
            for s in range(NS):
                pe.sem_inc(counted[s], 1)
            pe.sem_inc(feats, NU)
            pe.wait_ge(consts, NS + 1)
            for s in range(NS):
                nc.tensor.matmul(ps_cnt[s][:, 0:NB], ident[:, :], base[:, s, :], start=True, stop=False,
                                 skip_group_check=True)
            both_ways(pe, tensor_loop)

        @block.scalar
        def _(act):
            act.sem_inc(masked, 1)
            for s in range(NS):
                act.activation(free_rec[s][:, :], base[:, s, :], ACT.Copy).then_inc(next_ready[s], 1)
            both_ways(act, scalar_loop)


def spread(table, chunk):
    return table[bass.ds(chunk, 1), :].partition_broadcast(P).rearrange("p a e -> p (a e)")


def attend_stage(nc, T, x, rec_dram, out):
    iota_f, ident, q_tab, base, deg = (T[k] for k in ("iota_f", "ident", "q_tab", "base", "deg"))
    with ExitStack() as ctx:
        def sb(name, shape, dt=F32):
            return ctx.enter_context(nc.sbuf_tensor(name, shape, dt))

        def sem(name):
            return ctx.enter_context(nc.semaphore(name))

        more_dram = nc.dram_tensor("more_dram", (NB,), I32, kind="Internal").ap()
        start_i = sb("start_i", [P, NB], I32)
        most = sb("most", [NB, 1])
        more_i = sb("more_i", [NB, 1], I32)
        more = sb("more", [1, NB], I32)
        next_x = sb("next_x", [P, NB])
        left = sb("left", [P, NB])
        y = sb("y", [P, NB, DIM])
        spread_out = sb("spread_out", [P, 2, DIM])
        idx = [sb(f"idx{i}", [P, 1], I32) for i in range(RB)]
        rec = [sb(f"rec{i}", [P, S0, REC]) for i in range(RB)]
        neg = [sb(f"neg{i}", [P, H]) for i in range(RB)]
        den = [sb(f"den{i}", [P, H]) for i in range(RB)]
        qk = [sb(f"qk_s{i}", [P, S0, DH]) for i in range(2)]
        lg = [sb(f"lg{i}", [P, H, S0]) for i in range(2)]
        prob = [sb(f"prob{i}", [P, H, S0]) for i in range(2)]
        msg = [sb(f"msg{i}", [P, S0, DIM]) for i in range(2)]
        past = [sb(f"past{i}", [P, S0]) for i in range(2)]
        acc = [sb(f"acc{i}", [P, DIM]) for i in range(2)]
        idx_x = sb("idx_x", [P, 1], I32)
        rec_x = sb("rec_x", [P, SX, REC])
        qk_x = sb("qk_x", [P, SX, DH])
        lg_x = sb("lg_x", [P, H, SX])
        past_x = sb("past_x", [P, SX])
        prob_x = sb("prob_x", [P, H, SX])
        msg_x = sb("msg_x", [P, SX, DIM])
        neg_x, fall, fall_e, den_x = (sb(k, [P, H]) for k in ("neg_x", "fall", "fall_e", "den_x"))
        acc_x = sb("acc_x", [P, DIM])
        minus_mean = sb("minus_mean", [P, NB])
        rstd = sb("rstd", [P, NB])
        eps = sb("eps", [P, 1])
        ps_deg = ctx.enter_context(nc.psum_tensor("ps_deg", [NB, 512], F32))
        ps_sum = [ctx.enter_context(nc.psum_tensor(f"ps_sum{i}", [P, SUM, DIM], F32)) for i in range(2)]

        x_in, deg_up, more_made, more_out, more_in = (sem(n) for n in ("xs_in", "deg_up", "more_made", "more_out", "more_in"))
        ends, eps_set, rooted, normed, y_out = sem("ends"), sem("eps_set"), sem("rooted"), sem("normed"), sem("y_out")
        averaged, squared, centred = sem("averaged"), sem("squared"), sem("centred")
        rec_in = [sem(f"rec_in{i}") for i in range(RB)]
        idx_made, qk_made, dotted_all, with_edge, with_past, topped, maxed, expd, dve_spent, pool_spent, summed = (
            sem(n) for n in ("idx_made", "qk_made", "dotted_all", "with_edge", "with_past", "topped", "maxed", "expd",
                             "dve_spent", "pool_spent", "summed"))
        past_made, whole, den_safe, den_inv, scaled, added = (
            sem(n) for n in ("past_made", "whole", "den_safe", "den_inv", "scaled", "added"))
        xi_made, xr_in, x_maxed, x_expd, x_steps = (sem(n) for n in ("xi_made", "xr_in", "x_maxed", "x_expd", "x_steps"))
        gathers = sem("gathers")
        MORE = 16

        def steps(eng, step):
            for b in range(2):
                step(b, b, 0)
            with eng.Fori(0, (NB - 2 - RB) // RB) as it:
                for j in range(RB):
                    step(RB * it + 2 + j, 2 + j, it)
            for b in range(NB - RB, NB):
                step(b, b, 0)

        def is_last(b, n):
            return isinstance(b, int) and b >= NB - n

        def is_first(b, n):
            return isinstance(b, int) and b < n

        def by_head(t):
            return t.rearrange("p (h d) -> p h d", h=H)

        def further(eng, b, passes, one):
            m = eng.value_load(more[0:1, bass.ds(b, 1)], min_val=0, max_val=EP)
            with eng.If(m > 0):
                with eng.Fori(0, m):
                    one(eng.snap(passes))
                    eng.reg_add(passes, passes, 1)

        def count(eng, name):
            passes = eng.alloc_register(name)
            eng.reg_mov(passes, 0)
            return passes

        block = ctx.enter_context(nc.Block())

        @block.sync
        def _(sp):
            sp.dma_start(y[:, :, :], x.rearrange("(b p) f -> p b f", p=P)).then_inc(x_in, 16)
            sp.wait_ge(more_made, 1)
            sp.dma_start(more_dram.rearrange("(b a) -> b a", a=1), more_i[:, :]).then_inc(more_out, 16)
            sp.wait_ge(more_out, 16)
            sp.dma_start(more[:, :], row_of(more_dram)).then_inc(more_in, 16)
            full = N // P
            for g in range(NB // GN):
                sp.wait_ge(normed, g + 1)
                b0, b1 = g * GN, min((g + 1) * GN, full)
                sp.dma_start(out[b0 * P:b1 * P, :].rearrange("(b p) f -> p b f", p=P), y[:, b0:b1, :]).then_inc(y_out, 16)
            sp.dma_start(out[full * P:N, :], y[0:N - full * P, full, :]).then_inc(y_out, 16)
            sp.wait_ge(y_out, 16 * (NB // GN + 1))

        @block.gpsimd
        def _(pool):
            def gather(r, b):
                pool.indirect_dma_start(rec[r][:, :, :].rearrange("p s f -> p (s f)"), None, rec_dram[:, :],
                                        bass.IndirectOffsetOnAxis(idx[r][:, 0:1], 0)).then_inc(rec_in[r], 16)

            def products(r, b, turn):
                pool.wait_ge(rec_in[r], 16 * turn + 16)
                pool.tensor_tensor(qk[r % 2][:, :, :], rec[r][:, :, 0:DH],
                                   q_tab[:, bass.ds(b, 1), :].broadcast_to((P, S0, DH)), ALU.mult).then_inc(qk_made, 1)

            def step(b, j, turn):
                r = j % RB
                pool.wait_ge(expd, b + 1)
                if not is_first(b, 2):
                    pool.wait_ge(summed, b - 1)
                products_of_values(pool, rec[r], prob[r % 2], msg[r % 2], S0 - SP, S0).then_inc(pool_spent, 1)
                if not is_last(b, 2):
                    pool.wait_ge(maxed, b + 1)
                    products((j + 2) % RB, b + 2, turn + (j + 2) // RB)
                if not is_first(b, 2):
                    further(pool, b - 2, passes, gather_more)
                if not is_last(b, RB):
                    pool.wait_ge(idx_made, b + RB + 1)
                    pool.wait_ge(dve_spent, b + 1)
                    pool.wait_ge(pool_spent, b + 1)
                    pool.sem_inc(gathers, 1)
                    gather(r, b + RB)

            def gather_more(done):
                pool.wait_ge(xi_made, done + 1)
                pool.sem_inc(gathers, 1)
                pool.indirect_dma_start(rec_x[:, :, :].rearrange("p s f -> p (s f)"), None, rec_dram[:, :],
                                        bass.IndirectOffsetOnAxis(idx_x[:, 0:1], 0)).then_inc(xr_in, 16)

            for b in range(RB):
                pool.wait_ge(idx_made, b + 1)
                gather(b, b)
            products(0, 0, 0)
            products(1, 1, 0)
            pool.wait_ge(more_in, 16)
            passes = count(pool, "pool_passes")
            steps(pool, step)
            for b in range(NB - 2, NB):
                further(pool, b, passes, gather_more)

        @block.tensor
        def _(pe):
            nc.tensor.transpose(ps_deg[:, 0:P], deg[:, :], ident[:, :]).then_inc(deg_up, 1)

            def step(b, j, turn):
                i = j % 2
                pe.wait_ge(dve_spent, b + 1)
                pe.wait_ge(pool_spent, b + 1)
                for k in range(0, S0, SUM):
                    last = nc.tensor.matmul(ps_sum[i][:, :, :], ident[:, :], msg[i][:, k:k + SUM, :], start=(k == 0),
                                            stop=(k + SUM == S0))
                last.then_inc(summed, 1)

            steps(pe, step)

        @block.vector
        def _(dve):
            n = 0

            def end(ins):
                nonlocal n
                n += 1
                ins.then_inc(ends, 1)
                dve.wait_ge(ends, n)

            dve.memset(eps[:, :], 1e-5).then_inc(eps_set, 1)
            end(dve.tensor_copy(start_i[:, :], base[:, 0, :]))
            for b in range(RB):
                dve.tensor_copy(idx[b][:, :], start_i[:, b:b + 1]).then_inc(idx_made, 1)
            dve.wait_ge(deg_up, 1)
            end(dve.reduce_max(most[:, :], ps_deg[:, 0:P], AX.X))
            end(dve.tensor_scalar(most[:, :], most[:, :], float(SX - 1 - S0), 0.0, ALU.add, ALU.max))
            end(dve.tensor_copy(more_i[:, :], most[:, :]))
            dve.tensor_single_scalar(more_i[:, :], more_i[:, :], int(math.log2(SX)), ALU.arith_shift_right).then_inc(more_made, 1)
            end(dve.tensor_single_scalar(left[:, :], deg[:, :], -float(S0), ALU.add))
            end(dve.tensor_scalar(next_x[:, :], base[:, 0, :], float(S0), float(EP), ALU.add, ALU.min))
            dve.wait_ge(x_in, 16)

            def logit_ops(b, j):
                r, i = j % RB, j % 2
                by_slot = lg[i][:, :, :].rearrange("p h s -> p s h")

                def dot():
                    dve.tensor_scalar(past[i][:, :], iota_f[:, 0:S0], deg[:, bass.ds(b, 1)], -BIG, ALU.is_ge,
                                      ALU.mult).then_inc(past_made, 1)
                    dve.wait_ge(qk_made, b + 1)
                    dve.tensor_reduce(by_slot, qk[i][:, :, :].rearrange("p s (h d) -> p s h d", h=H), AX.X,
                                      ALU.add).then_inc(dotted_all, 1)

                def edge():
                    dve.wait_ge(dotted_all, b + 1)
                    dve.tensor_tensor(by_slot, by_slot, rec[r][:, :, KV:REC], ALU.add).then_inc(with_edge, 1)

                def beyond():
                    dve.wait_ge(with_edge, b + 1)
                    dve.wait_ge(past_made, b + 1)
                    dve.tensor_tensor(lg[i][:, :, :], lg[i][:, :, :], past[i][:, :].unsqueeze(1).broadcast_to((P, H, S0)),
                                      ALU.add).then_inc(with_past, 1)

                def top():
                    dve.wait_ge(with_past, b + 1)
                    dve.tensor_reduce(neg[r][:, :], lg[i][:, :, :], AX.X, ALU.max, negate=True).then_inc(topped, 1)

                def bound():
                    dve.wait_ge(topped, b + 1)
                    dve.tensor_single_scalar(neg[r][:, :], neg[r][:, :], BIG / 2, ALU.min).then_inc(maxed, 1)

                return dot, edge, beyond, top, bound

            def sum_ops(b, j):
                r, i = j % RB, j % 2
                row = y[:, bass.ds(b, 1), :].rearrange("p a f -> p (a f)")

                def gather_sums():
                    dve.wait_ge(summed, b + 1)
                    dve.tensor_reduce(acc[i][:, :], ps_sum[i][:, :, :].rearrange("p s f -> p f s"), AX.X,
                                      ALU.add).then_inc(whole, 1)

                def more_and_safe():
                    further(dve, b, passes, lambda done: one_more(b, r, i, done))
                    dve.tensor_single_scalar(den[r][:, :], den[r][:, :], 1e-16, ALU.add).then_inc(den_safe, 1)

                def invert():
                    dve.wait_ge(den_safe, b + 1)
                    dve.reciprocal(den[r][:, :], den[r][:, :]).then_inc(den_inv, 1)

                def scale():
                    dve.wait_ge(den_inv, b + 1)
                    dve.wait_ge(whole, b + 1)
                    dve.tensor_tensor(by_head(acc[i][:, :]), by_head(acc[i][:, :]),
                                      den[r][:, :].unsqueeze(2).broadcast_to((P, H, VD)), ALU.mult).then_inc(scaled, 1)

                def add():
                    dve.wait_ge(scaled, b + 1)
                    dve.tensor_tensor(row, acc[i][:, :], row, ALU.add).then_inc(added, 1)

                return gather_sums, more_and_safe, invert, scale, add

            def one_more(b, r, i, done):
                kx = 0

                def chain(ins):
                    nonlocal kx
                    kx += 1
                    ins.then_inc(x_steps, 1)
                    dve.wait_ge(x_steps, MORE * done + kx)

                at_b = bass.ds(b, 1)
                by_slot = lg_x[:, :, :].rearrange("p h s -> p s h")
                dve.wait_ge(whole, b + 1)
                dve.tensor_copy(idx_x[:, :], next_x[:, at_b]).then_inc(xi_made, 1)
                chain(dve.tensor_scalar(past_x[:, :], iota_f[:, 0:SX], left[:, at_b], -BIG, ALU.is_ge, ALU.mult))
                chain(dve.tensor_scalar(next_x[:, at_b], next_x[:, at_b], float(SX), float(EP), ALU.add, ALU.min))
                chain(dve.tensor_single_scalar(left[:, at_b], left[:, at_b], -float(SX), ALU.add))
                dve.wait_ge(xr_in, 16 * done + 16)
                chain(dve.tensor_tensor(qk_x[:, :, :], rec_x[:, :, 0:DH], q_tab[:, at_b, :].broadcast_to((P, SX, DH)), ALU.mult))
                chain(dve.tensor_reduce(by_slot, qk_x[:, :, :].rearrange("p s (h d) -> p s h d", h=H), AX.X, ALU.add))
                chain(dve.tensor_tensor(by_slot, by_slot, rec_x[:, :, KV:REC], ALU.add))
                chain(dve.tensor_tensor(lg_x[:, :, :], lg_x[:, :, :], past_x[:, :].unsqueeze(1).broadcast_to((P, H, SX)), ALU.add))
                chain(dve.tensor_reduce(neg_x[:, :], lg_x[:, :, :], AX.X, ALU.max, negate=True))
                chain(dve.tensor_tensor(neg_x[:, :], neg_x[:, :], neg[r][:, :], ALU.min))
                dve.tensor_tensor(fall[:, :], neg_x[:, :], neg[r][:, :], ALU.subtract).then_inc(x_maxed, 1)
                dve.wait_ge(x_maxed, done + 1)
                chain(dve.tensor_copy(neg[r][:, :], neg_x[:, :]))
                dve.wait_ge(x_expd, done + 1)
                chain(dve.tensor_tensor(den[r][:, :], den[r][:, :], fall_e[:, :], ALU.mult))
                chain(dve.tensor_tensor(den[r][:, :], den[r][:, :], den_x[:, :], ALU.add))
                chain(dve.tensor_tensor(by_head(acc[i][:, :]), by_head(acc[i][:, :]),
                                        fall_e[:, :].unsqueeze(2).broadcast_to((P, H, VD)), ALU.mult))
                chain(products_of_values(dve, rec_x, prob_x, msg_x, 0, SX))
                chain(dve.tensor_reduce(acc_x[:, :], msg_x[:, :, :].rearrange("p s f -> p f s"), AX.X, ALU.add))
                chain(dve.tensor_tensor(acc[i][:, :], acc[i][:, :], acc_x[:, :], ALU.add))
                assert kx == MORE, kx

            def step(b, j, turn):
                r, i = j % RB, j % 2
                nothing = (lambda: None,) * 5
                dot, edge, beyond, top, bound = nothing if is_last(b, 1) else logit_ops(b + 1, j + 1)
                gather_sums, more_and_safe, invert, scale, add = nothing if is_first(b, 2) else sum_ops(b - 2, j - 2)
                half = (S0 - SP) // 2
                gather_sums()
                dot()
                more_and_safe()
                dve.wait_ge(expd, b + 1)
                products_of_values(dve, rec[r], prob[i], msg[i], 0, half)
                edge()
                invert()
                products_of_values(dve, rec[r], prob[i], msg[i], half, S0 - SP).then_inc(dve_spent, 1)
                beyond()
                scale()
                if not is_last(b, RB):
                    dve.tensor_copy(idx[r][:, :], start_i[:, bass.ds(b + RB, 1)]).then_inc(idx_made, 1)
                top()
                add()
                bound()

            dve.wait_ge(more_in, 16)
            passes = count(dve, "dve_passes")
            for op in logit_ops(0, 0):
                op()
            steps(dve, step)
            for b in range(NB - 2, NB):
                for op in sum_ops(b, b):
                    op()
            dve.wait_ge(added, NB)

            dve.wait_ge(squared, NB)
            for g in range(NB // GN):
                rows = y[:, g * GN:(g + 1) * GN, :]
                dve.tensor_tensor(rows, rows, minus_mean[:, g * GN:(g + 1) * GN].unsqueeze(2).broadcast_to((P, GN, DIM)),
                                  ALU.add).then_inc(centred, 1)
            dve.wait_ge(rooted, 1)
            end(dve.reciprocal(rstd[:, :], rstd[:, :]))
            for g in range(NB // GN):
                rows = y[:, g * GN:(g + 1) * GN, :]
                dve.wait_ge(centred, g + 1)
                dve.tensor_tensor(rows, rows, rstd[:, g * GN:(g + 1) * GN].unsqueeze(2).broadcast_to((P, GN, DIM)),
                                  ALU.mult).then_inc(normed, 1)

        @block.scalar
        def _(act):
            def exps(p, logits, negated, total, done):
                for h in range(H):
                    last = act.activation(p[:, h, :], logits[:, h, :], ACT.Exp, bias=negated[:, h:h + 1],
                                          accum_out=total[:, h:h + 1])
                last.then_inc(done, 1)

            def softmax(b, j):
                act.wait_ge(maxed, b + 1)
                exps(prob[j % 2], lg[j % 2], neg[j % RB], den[j % RB], expd)

            def one_more(done):
                act.wait_ge(x_maxed, done + 1)
                act.activation(fall_e[:, :], fall[:, :], ACT.Exp)
                exps(prob_x, lg_x, neg_x, den_x, x_expd)

            def step(b, j, turn):
                if not is_first(b, 2):
                    further(act, b - 2, passes, one_more)
                if not is_last(b, 1):
                    softmax(b + 1, j + 1)
                if not is_first(b, 2):
                    statistics(b - 2)

            def statistics(b):
                row = y[:, bass.ds(b, 1), :].rearrange("p a f -> p (a f)")
                act.wait_ge(added, b + 1)
                act.activation(spread_out[:, 0, :], row, ACT.Copy, scale=-1.0 / DIM,
                               accum_out=minus_mean[:, bass.ds(b, 1)]).then_inc(averaged, 1)
                act.wait_ge(averaged, b + 1)
                act.activation(spread_out[:, 1, :], row, ACT.Square, bias=minus_mean[:, bass.ds(b, 1)],
                               accum_out=rstd[:, bass.ds(b, 1)]).then_inc(squared, 1)

            act.wait_ge(more_in, 16)
            passes = count(act, "act_passes")
            softmax(0, 0)
            steps(act, step)
            for b in range(NB - 2, NB):
                further(act, b, passes, one_more)
                statistics(b)
            act.wait_ge(eps_set, 1)
            act.wait_ge(squared, NB)
            act.activation(rstd[:, :], rstd[:, :], ACT.Sqrt, bias=eps[:, 0:1], scale=1.0 / DIM).then_inc(rooted, 1)


def products_of_values(eng, rec, prob, msg, s0, s1):
    return eng.tensor_tensor(
        msg[:, s0:s1, :].rearrange("p s (h d) -> p s h d", h=H),
        rec[:, s0:s1, DH:KV].rearrange("p s (h d) -> p s h d", h=H),
        prob[:, :, s0:s1].rearrange("p h s -> p s h").unsqueeze(3).broadcast_to((P, s1 - s0, H, VD)), ALU.mult)


def kernel(x, src, dst, edge_attr_18, L0_gnn_qkv_w, L0_gnn_qkv_b, L0_gnn_k_rpe_w, L0_gnn_k_rpe_b,
           L0_gnn_q_rpe_w, L0_gnn_q_rpe_b, L0_gnn_v_rpe_w, L0_gnn_v_rpe_b):
    import concourse.bacc as bacc
    from concourse.bass_utils import run_bass_kernel_spmd

    x, src, dst, attr = (np.asarray(a) for a in (x, src, dst, edge_attr_18))
    pad = (N + np.arange(EP - E) % (NN - N)).astype(np.int32)
    src = np.concatenate([src, pad])
    dst = np.concatenate([dst, pad])
    attr = np.concatenate([attr, np.zeros((EP - E, ATTR), attr.dtype)])
    x = np.concatenate([x, np.zeros((NN - N, DIM), x.dtype)])
    arrays = {
        "x": x,
        "xT": np.ascontiguousarray(x.T),
        "src_lin": src,
        "src_tiles": np.ascontiguousarray(src.reshape(NT, P).T),
        "dst_lin": dst,
        "dst_tiles": np.ascontiguousarray(dst.reshape(NT, P).T),
        "attr": np.ascontiguousarray(attr.reshape(NCH, CT, P, ATTR).transpose(0, 1, 3, 2)).reshape(NCH, CT * ATTR, P),
        "qkv_w": L0_gnn_qkv_w, "qkv_b": L0_gnn_qkv_b, "k_rpe_w": L0_gnn_k_rpe_w, "k_rpe_b": L0_gnn_k_rpe_b,
        "q_rpe_w": L0_gnn_q_rpe_w, "q_rpe_b": L0_gnn_q_rpe_b, "v_rpe_w": L0_gnn_v_rpe_w, "v_rpe_b": L0_gnn_v_rpe_b,
    }
    nc = bacc.Bacc("TRN2", target_bir_lowering=False, num_devices=1)
    feed, args = {}, []
    for name, a in arrays.items():
        a = np.ascontiguousarray(a)
        feed[f"in_{name}"] = a
        args.append(nc.dram_tensor(f"in_{name}", a.shape, mybir.dt.from_np(a.dtype), kind="ExternalInput").ap())
    args.append(nc.dram_tensor("out_y", (N, DIM), F32, kind="ExternalOutput").ap())
    gnn_kernel(nc, *args)
    r = run_bass_kernel_spmd(nc, [feed], core_ids=[0])
    return r.results[0]["out_y"]
```
